# Optimizing a Trainium2 kernel written in Bass

```python
import numpy as np
import jax
import jax.numpy as jnp

def _softmax(x, axis=-1):
    return jax.nn.softmax(x, axis=axis)

def _gelu(x):
    return jax.nn.gelu(x, approximate=True)

def _silu(x):
    return jax.nn.silu(x)

def _sigmoid(x):
    return jax.nn.sigmoid(x)

def _layernorm(x, axis=-1, eps=1e-05):
    m = jnp.mean(x, axis=axis, keepdims=True)
    v = jnp.var(x, axis=axis, keepdims=True)
    return (x - m) / jnp.sqrt(v + eps)

def _scatter_add(tgt, idx, src, axis=0):
    return tgt.at[idx].add(src)

def _segment_sum(src, seg, n):
    return jax.ops.segment_sum(src, seg, n)
kernel_name = 'mk_gnn_resnorm_d2_gnn_r8_fe63a2'

def setup_inputs(seed: int=0):
    np.random.seed(seed)
    _w = jnp.asarray

    def _rec_inputs():
        import jax
        import jax.numpy as jnp
        _gk = jax.random.key(seed)
        x = -0.0009044 + 1 * jax.random.normal(jax.random.fold_in(_gk, 1), (12500, 160), jnp.float32)
        src = jax.random.randint(jax.random.fold_in(_gk, 2), (200000,), 0, 12500, jnp.int32)
        dst = jax.random.randint(jax.random.fold_in(_gk, 3), (200000,), 0, 12500, jnp.int32)
        _o = jnp.argsort(dst, stable=True)
        src = src[_o]
        dst = dst[_o]
        edge_attr_16 = jax.random.uniform(jax.random.fold_in(_gk, 12), (200000, 16), jnp.float32, 0.0, 1)
        edge_attr_4 = -0.000149047 + 1.00006 * jax.random.normal(jax.random.fold_in(_gk, 13), (200000, 4), jnp.float32)
        edge_attr_8 = 0.000735704 + 1.0001 * jax.random.normal(jax.random.fold_in(_gk, 14), (200000, 8), jnp.float32)
        node_vec1 = jax.random.uniform(jax.random.fold_in(_gk, 15), (12500, 1), jnp.float32, 0.0, 1)
        return (x, src, dst, edge_attr_16, edge_attr_4, edge_attr_8, node_vec1)
    x, src, dst, edge_attr_16, edge_attr_4, edge_attr_8, node_vec1 = _rec_inputs()

    def _L0_gnn_setup():
        import jax, jax.numpy as jnp
        import numpy as np
        N_NODES = 1250
        N_EDGES = 40000
        NUM_NEIGHBORS = 32.0
        INV_SQRT3 = 1.0 / np.sqrt(3.0)

        def _fctp_scalar_attr(xs, xv, Ws, Wv, a):
            out_s = xs @ Ws * (a / np.sqrt(xs.shape[1]))[:, None]
            out_v = jnp.einsum('nuc,uw->nwc', xv, Wv) * (a / np.sqrt(xv.shape[1]))[:, None, None]
            return (out_s, out_v)
        key = jax.random.key(seed)
        ks = jax.random.split(key, 16)
        f32 = jnp.float32
        return {'node_input': jax.random.normal(ks[0], (N_NODES, 160), f32), 'node_attr': jnp.ones((N_NODES, 1), f32), 'edge_attr': jax.random.normal(ks[1], (N_EDGES, 4), f32), 'edge_scalar_attr': jax.random.normal(ks[2], (N_EDGES, 8), f32), 'Wsc0': jax.random.normal(ks[3], (64, 64), f32), 'Wsc1': jax.random.normal(ks[4], (32, 32), f32), 'Wl1_0': jax.random.normal(ks[5], (64, 64), f32), 'Wl1_1': jax.random.normal(ks[6], (32, 32), f32), 'Wfc1': jax.random.normal(ks[7], (8, 64), f32), 'Wfc2': jax.random.normal(ks[8], (64, 64), f32), 'Wfc3': jax.random.normal(ks[9], (64, 192), f32), 'Wl2_s': jax.random.normal(ks[10], (96, 64), f32), 'Wl2_v': jax.random.normal(ks[11], (96, 32), f32), 'Wa': jax.random.normal(ks[12], (96, 1), f32), 'edge_src': jax.random.randint(ks[13], (N_EDGES,), 0, N_NODES), 'edge_dst': jax.random.randint(ks[14], (N_EDGES,), 0, N_NODES)}
    _L0_gnn_all = _L0_gnn_setup()
    _L0_gnn_in = {k: v for k, v in _L0_gnn_all.items() if k in ('Wsc0', 'Wsc1', 'Wl1_0', 'Wl1_1', 'Wfc1', 'Wfc2', 'Wfc3', 'Wl2_s', 'Wl2_v', 'Wa')}
    del _L0_gnn_all

    def _L1_gnn_setup():
        import jax, jax.numpy as jnp
        import numpy as np
        import math
        N = 6250
        E = 62500
        MUL0 = 64
        MUL1 = 32
        MID = MUL0 + MUL1
        FC_IN = 16
        FC_H = 64
        WEIGHT_NUMEL = 2 * MUL0 + 2 * MUL1
        NUM_NEIGH = 10.0
        C_S = math.sin(math.pi / 8.0)
        C_X = math.cos(math.pi / 8.0)
        key = jax.random.key(seed)
        ks = jax.random.split(key, 14)
        f32 = jnp.float32
        return {'node_input': jax.random.normal(ks[0], (N, MUL0 + 3 * MUL1), f32), 'node_attr': jnp.ones((N, 1), f32), 'edge_src': jax.random.randint(ks[1], (E,), 0, N), 'edge_dst': jax.random.randint(ks[2], (E,), 0, N), 'edge_attr': jax.random.normal(ks[3], (E, 4), f32), 'edge_length_embedded': jax.random.uniform(ks[4], (E, FC_IN), dtype=f32), 'W_sc0': jax.random.normal(ks[5], (MUL0, MUL0), f32), 'W_sc1': jax.random.normal(ks[6], (MUL1, MUL1), f32), 'W_l1_0': jax.random.normal(ks[7], (MUL0, MUL0), f32), 'W_l1_1': jax.random.normal(ks[8], (MUL1, MUL1), f32), 'fc_W1': jax.random.normal(ks[9], (FC_IN, FC_H), f32), 'fc_W2': jax.random.normal(ks[10], (FC_H, WEIGHT_NUMEL), f32), 'W_l2_0': jax.random.normal(ks[11], (MID, MUL0), f32), 'W_l2_1': jax.random.normal(ks[12], (MID, MUL1), f32)}
    _L1_gnn_all = _L1_gnn_setup()
    _L1_gnn_in = {k: v for k, v in _L1_gnn_all.items() if k in ('W_sc0', 'W_sc1', 'W_l1_0', 'W_l1_1', 'fc_W1', 'fc_W2', 'W_l2_0', 'W_l2_1')}
    del _L1_gnn_all
    return {'x': x, 'src': src, 'dst': dst, 'edge_attr_16': edge_attr_16, 'edge_attr_4': edge_attr_4, 'edge_attr_8': edge_attr_8, 'node_vec1': node_vec1, 'L0_gnn_Wsc0': _L0_gnn_in['Wsc0'], 'L0_gnn_Wsc1': _L0_gnn_in['Wsc1'], 'L0_gnn_Wl1_0': _L0_gnn_in['Wl1_0'], 'L0_gnn_Wl1_1': _L0_gnn_in['Wl1_1'], 'L0_gnn_Wfc1': _L0_gnn_in['Wfc1'], 'L0_gnn_Wfc2': _L0_gnn_in['Wfc2'], 'L0_gnn_Wfc3': _L0_gnn_in['Wfc3'], 'L0_gnn_Wl2_s': _L0_gnn_in['Wl2_s'], 'L0_gnn_Wl2_v': _L0_gnn_in['Wl2_v'], 'L0_gnn_Wa': _L0_gnn_in['Wa'], 'L1_gnn_W_sc0': _L1_gnn_in['W_sc0'], 'L1_gnn_W_sc1': _L1_gnn_in['W_sc1'], 'L1_gnn_W_l1_0': _L1_gnn_in['W_l1_0'], 'L1_gnn_W_l1_1': _L1_gnn_in['W_l1_1'], 'L1_gnn_fc_W1': _L1_gnn_in['fc_W1'], 'L1_gnn_fc_W2': _L1_gnn_in['fc_W2'], 'L1_gnn_W_l2_0': _L1_gnn_in['W_l2_0'], 'L1_gnn_W_l2_1': _L1_gnn_in['W_l2_1']}

def reference(x, src, dst, edge_attr_16, edge_attr_4, edge_attr_8, node_vec1, L0_gnn_Wsc0, L0_gnn_Wsc1, L0_gnn_Wl1_0, L0_gnn_Wl1_1, L0_gnn_Wfc1, L0_gnn_Wfc2, L0_gnn_Wfc3, L0_gnn_Wl2_s, L0_gnn_Wl2_v, L0_gnn_Wa, L1_gnn_W_sc0, L1_gnn_W_sc1, L1_gnn_W_l1_0, L1_gnn_W_l1_1, L1_gnn_fc_W1, L1_gnn_fc_W2, L1_gnn_W_l2_0, L1_gnn_W_l2_1):
    import jax
    import jax.numpy as jnp

    def _L0_gnn_ref(node_input, node_attr, edge_attr, edge_scalar_attr, Wsc0, Wsc1, Wl1_0, Wl1_1, Wfc1, Wfc2, Wfc3, Wl2_s, Wl2_v, Wa, edge_src, edge_dst):
        import jax, jax.numpy as jnp
        import numpy as np
        N_NODES = 1250
        N_EDGES = 40000
        NUM_NEIGHBORS = 32.0
        INV_SQRT3 = 1.0 / np.sqrt(3.0)

        def _fctp_scalar_attr(xs, xv, Ws, Wv, a):
            out_s = xs @ Ws * (a / np.sqrt(xs.shape[1]))[:, None]
            out_v = jnp.einsum('nuc,uw->nwc', xv, Wv) * (a / np.sqrt(xv.shape[1]))[:, None, None]
            return (out_s, out_v)
        N = node_input.shape[0]
        a = node_attr[:, 0]
        xs = node_input[:, :64]
        xv = node_input[:, 64:].reshape(N, 32, 3)
        sc_s, sc_v = _fctp_scalar_attr(xs, xv, Wsc0, Wsc1, a)
        f_s, f_v = _fctp_scalar_attr(xs, xv, Wl1_0, Wl1_1, a)
        h = jax.nn.gelu(edge_scalar_attr @ Wfc1 / np.sqrt(8.0))
        h = jax.nn.gelu(h @ Wfc2 / np.sqrt(64.0))
        w = h @ Wfc3 / np.sqrt(64.0)
        w0, w1, w2, w3 = (w[:, :64], w[:, 64:128], w[:, 128:160], w[:, 160:192])
        gs = f_s[edge_src]
        gv = f_v[edge_src]
        y0 = edge_attr[:, 0]
        y1 = edge_attr[:, 1:4]
        mid0 = w0 * gs * y0[:, None]
        mid1 = w3 * jnp.einsum('euc,ec->eu', gv, y1) * INV_SQRT3
        mid2 = (w1 * gs)[:, :, None] * y1[:, None, :]
        mid3 = w2[:, :, None] * gv * y0[:, None, None]
        inv = 1.0 / np.sqrt(NUM_NEIGHBORS)
        seg = lambda x: jax.ops.segment_sum(x, edge_dst, num_segments=N) * inv
        ns0, ns1, nv2, nv3 = (seg(mid0), seg(mid1), seg(mid2), seg(mid3))
        mid_s = jnp.concatenate([ns0, ns1], axis=1)
        mid_v = jnp.concatenate([nv2, nv3], axis=1)
        out_s = mid_s @ Wl2_s * (a / np.sqrt(96.0))[:, None]
        out_v = jnp.einsum('nuc,uw->nwc', mid_v, Wl2_v) * (a / np.sqrt(96.0))[:, None, None]
        alpha = mid_s @ Wa * (a / np.sqrt(96.0))[:, None]
        res_s = sc_s + alpha * out_s
        res_v = sc_v + alpha[:, :, None] * out_v
        return jnp.concatenate([res_s, res_v.reshape(N, 96)], axis=1)

    def _L1_gnn_ref(node_input, node_attr, edge_src, edge_dst, edge_attr, edge_length_embedded, W_sc0, W_sc1, W_l1_0, W_l1_1, fc_W1, fc_W2, W_l2_0, W_l2_1):
        import jax, jax.numpy as jnp
        import numpy as np
        import math
        N = 6250
        E = 62500
        MUL0 = 64
        MUL1 = 32
        MID = MUL0 + MUL1
        FC_IN = 16
        FC_H = 64
        WEIGHT_NUMEL = 2 * MUL0 + 2 * MUL1
        NUM_NEIGH = 10.0
        C_S = math.sin(math.pi / 8.0)
        C_X = math.cos(math.pi / 8.0)
        n = node_input.shape[0]
        x0 = node_input[:, :MUL0]
        x1 = node_input[:, MUL0:].reshape(n, MUL1, 3)
        a = node_attr
        inv0 = 1.0 / math.sqrt(MUL0)
        inv1 = 1.0 / math.sqrt(MUL1)
        s0 = x0 @ W_sc0 * a * inv0
        s1 = jnp.einsum('nuc,uv->nvc', x1, W_sc1) * a[:, :, None] * inv1
        y0 = x0 @ W_l1_0 * a * inv0
        y1 = jnp.einsum('nuc,uv->nvc', x1, W_l1_1) * a[:, :, None] * inv1
        h = jax.nn.silu(edge_length_embedded @ fc_W1 * (1.0 / math.sqrt(FC_IN)))
        w = h @ fc_W2 * (1.0 / math.sqrt(FC_H))
        w_a = w[:, :MUL0]
        w_b = w[:, MUL0:2 * MUL0]
        w_c = w[:, 2 * MUL0:2 * MUL0 + MUL1]
        w_d = w[:, 2 * MUL0 + MUL1:]
        ys0 = y0[edge_src]
        ys1 = y1[edge_src]
        e0 = edge_attr[:, :1]
        e1 = edge_attr[:, 1:]
        mid_a = w_a * ys0 * e0
        mid_d = w_d * jnp.einsum('euc,ec->eu', ys1, e1) * (1.0 / math.sqrt(3.0))
        mid_b = (w_b * ys0)[:, :, None] * e1[:, None, :]
        mid_c = (w_c * e0)[:, :, None] * ys1
        mid0 = jnp.concatenate([mid_a, mid_d], axis=1)
        mid1 = jnp.concatenate([mid_b, mid_c], axis=1)
        inv_nb = 1.0 / math.sqrt(NUM_NEIGH)
        z0 = jnp.zeros((n, MID), mid0.dtype).at[edge_dst].add(mid0) * inv_nb
        z1 = jnp.zeros((n, MID, 3), mid1.dtype).at[edge_dst].add(mid1) * inv_nb
        inv_mid = 1.0 / math.sqrt(MID)
        o0 = z0 @ W_l2_0 * a * inv_mid
        o1 = jnp.einsum('nuc,uv->nvc', z1, W_l2_1) * a[:, :, None] * inv_mid
        out0 = C_S * s0 + C_X * o0
        out1 = C_S * s1 + C_X * o1
        return jnp.concatenate([out0, out1.reshape(n, MUL1 * 3)], axis=1)
    x = _layernorm(x + _L0_gnn_ref(x, node_vec1, edge_attr_4, edge_attr_8, L0_gnn_Wsc0, L0_gnn_Wsc1, L0_gnn_Wl1_0, L0_gnn_Wl1_1, L0_gnn_Wfc1, L0_gnn_Wfc2, L0_gnn_Wfc3, L0_gnn_Wl2_s, L0_gnn_Wl2_v, L0_gnn_Wa, src, dst), axis=-1)
    x = _layernorm(x + _L1_gnn_ref(x, node_vec1, src, dst, edge_attr_4, edge_attr_16, L1_gnn_W_sc0, L1_gnn_W_sc1, L1_gnn_W_l1_0, L1_gnn_W_l1_1, L1_gnn_fc_W1, L1_gnn_fc_W2, L1_gnn_W_l2_0, L1_gnn_W_l2_1), axis=-1)
    return x

_drawn_inputs = setup_inputs


def setup_inputs(seed=0):
    import zlib

    import numpy as np

    out = dict(_drawn_inputs(seed))
    spreads = {}
    factors = {'edge_attr_8': 5.365,
     'L0_gnn_Wl1_0': 5.501,
     'L0_gnn_Wl1_1': 6.372,
     'L0_gnn_Wfc1': 5.657,
     'L0_gnn_Wfc2': 5.289,
     'L0_gnn_Wfc3': 5.243,
     'L0_gnn_Wl2_s': 8.0,
     'L0_gnn_Wl2_v': 6.684,
     'L0_gnn_Wa': 4.791}
    for name, (base, spread) in spreads.items():
        noise = np.random.default_rng([zlib.crc32(name.encode()), seed]).standard_normal(out[name].shape)
        drawn = base * np.exp(spread * noise) if base else spread * noise
        out[name] = jnp.asarray(drawn.astype(out[name].dtype))
    for name, factor in factors.items():
        out[name] = (out[name] * factor).astype(out[name].dtype)
    return out
```

```python
from contextlib import ExitStack

import concourse.bass as bass
from concourse import mybir

F32 = mybir.dt.float32
I32 = mybir.dt.int32
ALU = mybir.AluOpType
ACT = mybir.ActivationFunctionType
AXX = mybir.AxisListType.X

P = 128
N_NODES, N_EDGES = 12500, 200000
MS, MV = 64, 32
DV, D = 3 * MV, 3 * MV + MS
TILES = 8
PAIRS = TILES // 2
SLOTS = P // TILES
GROUP = TILES * P
GROUPS = -(-N_EDGES // GROUP)
UNROLL = 4
HID = GROUP // 2
NT = -(-N_NODES // P)
CH = 7
CHUNKS = NT // CH
ROWS = P * NT + P
TRASH = P * NT
ZW = D + 1
NI = 3 * TILES + 1
XS = D + 1
EPS = 1e-5
assert GROUPS % UNROLL == 0 and NT % CH == 0 and CHUNKS % 2 == 0 and P * NT >= N_NODES + SLOTS - 1

W_NODEV, W_NODES, W_H1, W_H2, W_W3 = 0, 2 * DV, 2 * DV + 2 * MS, 2 * D + P, 2 * D + 2 * P
W_ZA1 = W_W3 + 2 * 192
W_ZA2 = W_ZA1 + MV + MS + 1
W_ZB = W_ZA2 + 2 * MV
W_ZC = W_ZB + DV
W_END = W_ZC + MS + 1
C_SLOT, C_PMOD, C_TRASH, C_LOWER, C_IDENT = 0, SLOTS, SLOTS + 1, SLOTS + 2, SLOTS + 2 + P
C_END = C_IDENT + P


class Layer:

    def __init__(self, n, w, ea, attrs):
        self.n, self.w, self.ea, self.attrs = n, w, ea, attrs
        self.deep = n == 0
        self.kappa = (1 / 8) * (96 ** -0.5) * ((32 ** -0.5) if n == 0 else (10 ** -0.5) * COS)


COS, SIN = 0.9238795325112867, 0.3826834323650898


def build(nc, dram):
    layers = [Layer(0, dram["w0"], dram["ea8"], 8), Layer(1, dram["w1"], dram["ea16"], 16)]
    f_dram = [nc.dram_tensor(f"f{l}", (P * NT, D), F32).ap() for l in range(2)]
    acc_dram = [nc.dram_tensor(f"acc{l}", (ROWS, ZW), F32).ap() for l in range(2)]
    x_in = dram["x"].rearrange("(p k) n -> p k n", k=NT)
    out_v = dram["out"].rearrange("(p k) n -> p k n", k=NT)
    f_v = [f.rearrange("(p k) n -> p k n", k=NT) for f in f_dram]
    acc_v = [a[0:P * NT, :].rearrange("(p k) n -> p k n", k=NT) for a in acc_dram]

    with ExitStack() as ctx:
        def sb(name, shape, dt=F32):
            return ctx.enter_context(nc.sbuf_tensor(name, shape, dt))

        def sem(name):
            return ctx.enter_context(nc.semaphore(name))

        bank = [ctx.enter_context(nc.psum_tensor(f"bank{i}", [P, 512], F32)) for i in range(8)]
        aggA_ps, aggB_ps, aggC_ps, hid1_ps, hid2_ps, z_ps = bank[0], bank[1], bank[2], bank[5], bank[6], bank[7]
        w_ps = bank[3:5]

        consts = sb("consts", [P, C_END])
        wt = [sb(f"weights{l}", [P, W_END]) for l in range(2)]
        base = sb("base", [P, NT * XS])
        ints = sb("ints", [P, UNROLL, NI], I32)
        ysb = sb("ysb", [P, UNROLL, TILES, 4])
        ea = sb("ea", [P, UNROLL, HID])
        h1 = sb("h1", [P, HID])
        h2 = sb("h2", [P, 2, HID])
        gath = sb("gath", [P, UNROLL, TILES, D])
        prod = sb("prod", [P, 2, 2, 320])
        sel = sb("sel", [P, 2, TILES, 4, SLOTS])
        rel = sb("rel", [P, TILES])
        onehot = sb("onehot", [P, TILES, SLOTS])
        slot_row = sb("slot_row", [P, TILES, SLOTS])
        slot_col = sb("slot_col", [P, 1])
        same = sb("same", [P, 2, P])
        earlier = sb("earlier", [P, P])
        dup = sb("dup", [P, 1])
        is_dup = sb("is_dup", [P, 1])
        to_trash = sb("to_trash", [P, 1])
        target = sb("target", [P, UNROLL, 1], I32)
        zA1, zA2, zB, zC = (sb(n, [P, P]) for n in ("zA1", "zA2", "zB", "zC"))
        zrow = sb("zrow", [P, ZW])
        zsum = sb("zsum", [P, UNROLL, ZW])
        xvT = sb("xvT", [DV, 2, CH, P])
        xsT = sb("xsT", [MS, 2, CH, P])
        rows_in = sb("rows_in", [P, 2, CH, XS])
        two = sb("two", [P, 2, CH, 2, D])
        resid = sb("resid", [P, CH, D])
        xn = sb("xn", [P, 2, CH, D])
        tvT = sb("tvT", [DV, 2, P])
        tsT = sb("tsT", [MS, 2, P])
        attr = sb("attr", [P, 2, CH])
        gain = sb("gain", [P, CH])
        stats = sb("stats", [P, CH, 6])
        mv = sb("mv", [P, CH, 2])
        std = sb("std", [P, CH])
        rstd = sb("rstd", [P, CH])
        zeros = sb("zeros", [P, 3 * ZW])
        base3 = base[:, :].rearrange("p (k n) -> p k n", n=XS)
        dst_all = sb("dst_all", [P, GROUPS * TILES], I32)
        first_all = sb("first_all", [P, GROUPS * TILES], I32)
        worst = sb("worst", [P, 4])
        ones = sb("ones", [P, 1])
        flag = sb("flag", [P, 1], I32)
        wide = sb("wide", [P, 4, P])
        dst_row = sb("dst_row", [P, P])
        spread = sb("spread", [P, P])

        s = {n: sem(n) for n in (
            "consts_in", "memsets", "weights_in", "weights_scaled", "acc_zeroed", "dst_in", "span_step",
            "span_sum", "flag_set", "tick")}
        ns = [{n: sem(f"n{k}_{n}") for n in (
            "in0", "in1", "transposed", "turned", "psum", "made", "base", "out0", "out1",
            "step", "variance", "rooted", "normed")} for k in range(3)]
        es = []
        for l in range(2):
            e = {n: sem(f"e{l}_{n}") for n in (
                "l1", "h1", "l2", "h2", "w", "prods", "scattered", "evacAB", "evacC", "prep",
                "projected", "z", "combined", "zsum", "added", "tick", "done", "turn", "g_gathered")}
            e["loaded"] = [sem(f"e{l}_loaded{b}") for b in range(UNROLL)]
            e["ea_in"] = [sem(f"e{l}_ea_in{b}") for b in range(UNROLL)]
            e["gathered"] = [sem(f"e{l}_gathered{b}") for b in range(UNROLL)]
            es.append(e)
        block = ctx.enter_context(nc.Block())

        class G:

            def __init__(self, i, c):
                self.i, self.c = i, c
                self.b = c % UNROLL

            def times(self, k, plus):
                return self.c * k + plus if self.i is None else self.i * (UNROLL * k) + (self.c * k + plus)

            def slot_count(self, per):
                q = self.c // UNROLL * per + per
                return q if self.i is None else self.i * per + q

            def has(self, lo):
                return self.i is not None or 0 <= self.c + lo < GROUPS

            def at(self):
                return bass.ds(self.c, 1) if self.i is None else bass.ds(self.i * UNROLL + self.c, 1)

        def groups(eng, body):
            for c in range(UNROLL):
                body(G(None, c))
            with eng.Fori(1, GROUPS // UNROLL - 1) as i:
                for c in range(UNROLL):
                    body(G(i, c))
            for c in range(GROUPS - UNROLL, GROUPS):
                body(G(None, c))

        def c_(a, n):
            return consts[:, a:a + n]

        def turns(deep):
            order = ["l1", "h1"] + (["l2", "h2"] if deep else [])
            for q in range(PAIRS):
                order += [f"w{q}", f"prod{q}"]
                for h in range(2):
                    order += [f"{k}{2 * q + h}" for k in (
                        "spread", "drow", "prep", "prep_b", "prep_c", "prep_d", "target", "scatter", "evac", "project", "z", "combine", "zsum", "add")]
            return {n: k for k, n in enumerate(order)}, len(order)

        def edge_loads(sp, L):
            e = es[L.n]

            def body(g):
                b = g.b
                if g.i is not None or g.c >= UNROLL:
                    sp.wait_ge(e["prods"], g.times(PAIRS, -PAIRS * (UNROLL - 1)))
                    sp.sem_inc(e["tick"], 1)
                sp.dma_start(ints[:, b, :], dram["ints"][g.at()].rearrange("a p n -> (a p) n")).then_inc(e["loaded"][b], 16)
                sp.dma_start(ysb[:, b], dram["y"][g.at()].rearrange("a p t c -> (a p) t c")).then_inc(e["loaded"][b], 16)
                sp.dma_start(ea[0:2 * L.attrs, b, :], L.ea[g.at()].rearrange("a r n -> (a r) n")).then_inc(e["ea_in"][b], 16)
            groups(sp, body)

        def edge_loads_general(sp, L):
            e = es[L.n]
            _, n = turns(L.deep)
            sp.sem_inc(e["turn"], 1)
            with sp.Fori(0, GROUPS) as i:
                sp.wait_ge(e["turn"], i * n + 1)
                sp.sem_inc(e["tick"], 1)
                sp.dma_start(ints[:, 0, :], dram["ints"][bass.ds(i, 1)].rearrange("a p n -> (a p) n")).then_inc(e["loaded"][0], 16)
                sp.dma_start(ysb[:, 0], dram["y"][bass.ds(i, 1)].rearrange("a p t c -> (a p) t c")).then_inc(e["loaded"][0], 16)
                sp.dma_start(ea[0:2 * L.attrs, 0, :], L.ea[bass.ds(i, 1)].rearrange("a r n -> (a r) n")).then_inc(e["loaded"][0], 16)

        def choose(eng, fast, general):
            v = eng.value_load(flag[0:1, 0:1], min_val=0, max_val=1)
            with eng.If(v):
                fast()
            with eng.Else():
                general()

        def chunks(eng, body):
            for b in range(2):
                body(0, b)
            with eng.Fori(1, CHUNKS // 2) as j:
                for b in range(2):
                    body(j * 2, b)

        def later(i):
            return not isinstance(i, int)

        def chunk_cols(i, b):
            return bass.ds((i + b) * CH, CH)

        @block.sync
        def _(sp):
            sp.dma_start(consts[:, :], dram["consts"]).then_inc(s["consts_in"], 16)
            sp.dma_start(dst_all[:, :], dram["dst_all"]).then_inc(s["dst_in"], 16)
            sp.dma_start(first_all[:, :], dram["first_all"]).then_inc(s["dst_in"], 16)
            n0 = ns[0]

            def load0(i, b):
                if later(i):
                    sp.wait_ge(n0["base"], i * 2 + 2 * (b - 1))
                    sp.sem_inc(s["tick"], 1)
                k = chunk_cols(i, b)
                sp.dma_start(xvT[:, b], dram["xvT"][:, k, :]).then_inc(n0[f"in{b}"], 16)
                sp.dma_start(xsT[:, b], dram["xsT"][:, k, :]).then_inc(n0[f"in{b}"], 16)
                sp.dma_start(rows_in[:, b], x_in[:, k, :]).then_inc(n0[f"in{b}"], 16)
            chunks(sp, load0)
            sp.wait_ge(s["memsets"], 1)
            for l in range(2):
                for r in range(0, ROWS, 3 * P):
                    sp.dma_start(acc_dram[l][r:r + 3 * P, :].rearrange("(p k) n -> p (k n)", k=3),
                                 zeros[:, :]).then_inc(s["acc_zeroed"], 16)
            sp.wait_ge(s["flag_set"], 1)
            for l in range(2):
                choose(sp, lambda: edge_loads(sp, layers[l]), lambda: edge_loads_general(sp, layers[l]))
                n = ns[l + 1]
                sp.wait_ge(n0["base"], 2 * CHUNKS)
                sp.wait_ge(es[l]["done"], 1)

                def load(i, b):
                    if later(i):
                        sp.wait_ge(n["variance"], i + (b - 1))
                        sp.sem_inc(s["tick"], 1)
                    sp.dma_start(rows_in[:, b], acc_v[l][:, chunk_cols(i, b), :]).then_inc(n[f"in{b}"], 16)
                chunks(sp, load)
            for b in range(2):
                sp.wait_ge(ns[2][f"out{b}"], 16 * (CHUNKS // 2))

        def gather_tile(g_out, idx, l, done):
            nc.gpsimd.indirect_dma_start(g_out, None, f_dram[l][:, :],
                                         bass.IndirectOffsetOnAxis(ap=idx, axis=0)).then_inc(done, 16)

        def add_rows(l, idx, rows, done):
            nc.gpsimd.indirect_dma_start(acc_dram[l][:, :], bass.IndirectOffsetOnAxis(ap=idx, axis=0),
                                         rows, None, compute_op=ALU.add).then_inc(done, 16)

        ADD_LAG = UNROLL + 1

        def edge_pool(pool, L):
            e = es[L.n]

            def wait(sem_, value):
                pool.wait_ge(sem_, value)
                pool.sem_inc(e["tick"], 1)

            def add(g):
                wait(e["zsum"], g.times(1, 1))
                if g.i is not None or g.c >= 1:
                    wait(e["added"], g.times(16, 0))
                add_rows(L.n, target[:, g.b, :], zsum[:, g.b, :], e["added"])

            def body(g):
                b = g.b
                wait(e["loaded"][b], g.slot_count(32))
                if g.i is not None or g.c >= UNROLL:
                    wait(e["prods"], g.times(PAIRS, -PAIRS * (UNROLL - 1)))
                for t in range(TILES):
                    gather_tile(gath[:, b, t, :], ints[:, b, t:t + 1], L.n, e["gathered"][b])
                if g.i is not None or g.c >= ADD_LAG:
                    add(G(g.i, g.c - ADD_LAG))
            for c in range(2 * UNROLL):
                body(G(None, c))
            with pool.Fori(2, GROUPS // UNROLL) as i:
                for c in range(UNROLL):
                    body(G(i, c))
            for c in range(GROUPS - ADD_LAG, GROUPS):
                add(G(None, c))
            pool.wait_ge(e["added"], 16 * GROUPS)
            pool.sem_inc(e["done"], 1)

        def edge_pool_general(pool, L):
            e = es[L.n]
            at, n = turns(L.deep)
            with pool.Fori(0, GROUPS) as i:
                pool.wait_ge(e["loaded"][0], i * 48 + 48)
                pool.sem_inc(e["tick"], 1)
                for t in range(TILES):
                    gather_tile(gath[:, 0, t, :], ints[:, 0, t:t + 1], L.n, e["g_gathered"])
                for t in range(TILES):
                    pool.wait_ge(e["turn"], i * n + (1 + at[f"add{t}"]))
                    pool.sem_inc(e["tick"], 1)
                    add_rows(L.n, target[:, 0, :], zsum[:, 0, :], e["added"])
                    pool.wait_ge(e["added"], i * (16 * TILES) + 16 * (t + 1))
                    pool.sem_inc(e["turn"], 1)
            pool.sem_inc(e["done"], 1)

        BASE_STEPS = (2, 1)

        def base_rows(pool, k, own):
            n = ns[k]

            def body(i, b):
                if k == 0:
                    pool.wait_ge(n[f"in{b}"], i * 24 + 48)
                    nc.gpsimd.tensor_copy(base3[:, chunk_cols(i, b), D:XS], rows_in[:, b, :, D:XS]).then_inc(n["base"], 1)
                pool.wait_ge(n["made"], i * CH + (b + 1) * CH)
                nc.gpsimd.tensor_tensor(base3[:, chunk_cols(i, b), 0:D], two[:, b, :, 1, :], own(b),
                                        ALU.add).then_inc(n["base"], 1)
            chunks(pool, body)

        @block.gpsimd
        def _(pool):
            base_rows(pool, 0, lambda b: rows_in[:, b, :, 0:D])
            pool.wait_ge(s["acc_zeroed"], 16 * 2 * (ROWS // P // 3))
            pool.wait_ge(s["flag_set"], 1)
            for l in range(2):
                if l == 1:
                    base_rows(pool, 1, lambda b: xn[:, b])
                for b in range(2):
                    pool.wait_ge(ns[l][f"out{b}"], 16 * (CHUNKS // 2))
                choose(pool, lambda: edge_pool(pool, layers[l]), lambda: edge_pool_general(pool, layers[l]))

        def evacA(ps, cols):
            yield zA1[0:64, :], cols(ps[0:64, :], 0)
            yield zA1[64:128, :], cols(ps[64:128, :], 3)
            yield zA2[0:64, :], cols(ps[64:128, :], 1)
            yield zA2[64:128, :], cols(ps[64:128, :], 2)

        def narrow(ps, c):
            return ps.rearrange("p (t c j) -> p t c j", c=4, j=SLOTS)[:, :, c, :]

        def broad(ps, c):
            return ps[:, c * P:(c + 1) * P]

        def as_slots(out, cols):
            return out.rearrange("p (t j) -> p t j", j=SLOTS) if cols is narrow else out

        def evac_A_and_B(act, cols, done, each=True):
            todo = list(evacA(aggA_ps, cols)) + [(zB[0:DV, :], cols(aggB_ps[0:DV, :], 0))]
            for n, (o, i) in enumerate(todo):
                ins = nc.scalar.activation(as_slots(o, cols), i, ACT.Copy)
                if each or n == len(todo) - 1:
                    ins.then_inc(done, 1)

        def evac_C(copy, cols):
            for c in range(3):
                ins = copy(as_slots(zC[32 * c:32 * c + 32, :], cols), cols(aggC_ps[32 * c:32 * c + 32, :], c + 1))
            return ins

        def activate1(L, out):
            func = ACT.Gelu_apprx_tanh if L.deep else ACT.Silu
            return nc.scalar.activation(out, hid1_ps[:, :], func, scale=(2 * L.attrs / 2) ** -0.5)

        def activate2(out):
            return nc.scalar.activation(out, hid2_ps[:, :], ACT.Gelu_apprx_tanh, scale=MS ** -0.5)

        def edge_act(act, L):
            e = es[L.n]

            def hidden1(g):
                act.wait_ge(e["l1"], g.times(1, 1))
                if L.deep:
                    if g.has(-1):
                        act.wait_ge(e["l2"], g.times(1, 0))
                    activate1(L, h1[:, :]).then_inc(e["h1"], 1)
                else:
                    if g.has(-2):
                        act.wait_ge(e["w"], g.times(PAIRS, -PAIRS))
                    activate1(L, h2[:, g.b % 2, :]).then_inc(e["h2"], 1)

            def hidden2(g):
                act.wait_ge(e["l2"], g.times(1, 1))
                if g.has(-2):
                    act.wait_ge(e["w"], g.times(PAIRS, -PAIRS))
                activate2(h2[:, g.b % 2, :]).then_inc(e["h2"], 1)

            def evacuate(g):
                act.wait_ge(e["scattered"], g.times(PAIRS, PAIRS))
                if g.has(-1):
                    act.wait_ge(e["projected"], g.times(1, 0))
                evac_A_and_B(act, narrow, e["evacAB"])

            def zrows(g):
                act.wait_ge(e["projected"], g.times(1, 1))
                if g.has(-1):
                    act.wait_ge(e["combined"], g.times(1, 0))
                nc.scalar.activation(zrow[:, :], z_ps[:, 0:ZW], ACT.Copy).then_inc(e["z"], 1)

            def zsums(g):
                act.wait_ge(e["combined"], g.times(1, 1))
                if g.i is not None or g.c >= UNROLL:
                    act.wait_ge(e["added"], g.times(16, -16 * (UNROLL - 1)))
                nc.scalar.activation(zsum[:, g.b, :], z_ps[:, 0:ZW], ACT.Copy).then_inc(e["zsum"], 1)

            def body(g):
                before, after = G(g.i, g.c - 1), G(g.i, g.c + 1)
                if g.has(-1):
                    evacuate(before)
                if g.has(1):
                    hidden1(after)
                if g.has(-1):
                    zrows(before)
                if g.has(1) and L.deep:
                    hidden2(after)
                if g.has(-1):
                    zsums(before)
            hidden1(G(None, 0))
            if L.deep:
                hidden2(G(None, 0))
            groups(act, body)
            last = G(None, GROUPS - 1)
            evacuate(last)
            zrows(last)
            zsums(last)

        def edge_act_general(act, L):
            e = es[L.n]
            at, n = turns(L.deep)
            with act.Fori(0, GROUPS) as i:
                def turn(name):
                    act.wait_ge(e["turn"], i * n + (1 + at[name]))
                turn("h1")
                activate1(L, h1[:, :] if L.deep else h2[:, 0, :]).then_inc(e["turn"], 1)
                if L.deep:
                    turn("h2")
                    activate2(h2[:, 0, :]).then_inc(e["turn"], 1)
                for t in range(TILES):
                    turn(f"evac{t}")
                    evac_C(lambda o, x: nc.scalar.activation(o, x, ACT.Copy), broad)
                    evac_A_and_B(act, broad, e["turn"], each=False)
                    turn(f"z{t}")
                    nc.scalar.activation(zrow[:, :], z_ps[:, 0:ZW], ACT.Copy).then_inc(e["turn"], 1)
                    turn(f"zsum{t}")
                    nc.scalar.activation(zsum[:, 0, :], z_ps[:, 0:ZW], ACT.Copy).then_inc(e["turn"], 1)

        def scaled_rows(act, k, l, attribute, turn_over):
            n = ns[k]

            def body(i, b):
                if later(i):
                    act.wait_ge(n[f"out{b}"], i * 8)
                    act.wait_ge(n["base"], i * BASE_STEPS[k] + BASE_STEPS[k] * (b - 1))
                    act.sem_inc(s["tick"], 1)
                for j in range(CH):
                    tile = b * CH + j
                    if turn_over:
                        turn_over(i, tile, 0 if j == 0 else 1)
                    act.wait_ge(n["psum"], i * CH + (tile + 1))
                    nc.scalar.activation(two[:, b, j].rearrange("p a n -> p (a n)"), bank[3 + tile % 2][:, 0:2 * D],
                                         ACT.Copy, scale=attribute(b, j)).then_inc(n["made"], 1)
                act.wait_ge(n["made"], i * CH + (b + 1) * CH)
                act.sem_inc(s["tick"], 1)
                act.dma_start(f_v[l][:, chunk_cols(i, b), :], two[:, b, :, 0, :]).then_inc(n[f"out{b}"], 16)
            return body

        def root(act, n, i, b):
            act.wait_ge(n["variance"], i + (b + 1))
            nc.scalar.activation(std[:, :], std[:, :], ACT.Sqrt).then_inc(n["rooted"], 1)

        def load_weights(eng, l):
            w, name = wt[l], (lambda k: dram[f"w{l}"][k])

            def put(r, c, k, rows=slice(None)):
                src = name(k)[rows, :]
                eng.dma_start(w[r:r + src.shape[0], c:c + src.shape[1]], src).then_inc(s["weights_in"], 16)
            for v in range(3):
                put(MV * v, W_NODEV + MV * v, "l1_v")
                put(MV * v, W_NODEV + DV + MV * v, "sc_v")
                put(MV * v, W_ZB + MV * v, "l2_v", slice(MS, MS + MV))
                put(MV * v, W_ZC, "l2_s", slice(MS, MS + MV))
                if l == 0:
                    put(MV * v, W_ZC + MS, "a", slice(MS, MS + MV))
            put(0, W_NODES, "l1_s")
            put(0, W_NODES + MS, "sc_s")
            for h in range(2):
                put(layers[l].attrs * h, W_H1 + MS * h, "h1")
                if layers[l].deep:
                    put(MS * h, W_H2 + MS * h, "h2")
                put(MS * h, W_W3 + 192 * h, "w3")
                put(64 * h, W_ZA2 + MV * h, "l2_v", slice(0, MS))
            put(64, W_ZA1, "l2_v", slice(0, MS))
            put(0, W_ZA1 + MV, "l2_s", slice(0, MS))
            if l == 0:
                put(0, W_ZA1 + MV + MS, "a", slice(0, MS))

        WEIGHT_DMAS = (12 + 3 + 2 + 2 * 4 + 3) + (12 + 2 + 2 * 3 + 2)

        @block.scalar
        def _(act):
            act.wait_ge(s["memsets"], 1)
            load_weights(act, 0)
            load_weights(act, 1)
            chunks(act, scaled_rows(act, 0, 0, lambda b, j: rows_in[:, b, j, D:XS], None))
            act.wait_ge(s["flag_set"], 1)
            choose(act, lambda: edge_act(act, layers[0]), lambda: edge_act_general(act, layers[0]))

            n1 = ns[1]

            def turn_over(i, tile, _):
                act.wait_ge(n1["transposed"], i * CH + (tile + 1))
                if later(i) or tile >= 2:
                    act.wait_ge(n1["psum"], i * CH + (tile - 1))
                nc.scalar.activation(tvT[:, tile % 2, :], bank[5 + tile % 2][0:DV, 0:P], ACT.Copy)
                nc.scalar.activation(tsT[:, tile % 2, :], bank[5 + tile % 2][0:MS, P:2 * P],
                                     ACT.Copy).then_inc(n1["turned"], 1)
            rows1 = scaled_rows(act, 1, 1, lambda b, j: attr[:, b, j:j + 1], turn_over)

            def body1(i, b):
                root(act, n1, i, b)
                rows1(i, b)
            chunks(act, body1)
            choose(act, lambda: edge_act(act, layers[1]), lambda: edge_act_general(act, layers[1]))

            n2 = ns[2]

            def body2(i, b):
                root(act, n2, i, b)
                act.wait_ge(n2["normed"], i + (b + 1))
                act.sem_inc(s["tick"], 1)
                act.dma_start(out_v[:, chunk_cols(i, b), :], xn[:, b]).then_inc(n2[f"out{b}"], 16)
            chunks(act, body2)

        def mm(out, lhsT, rhs, start=True, stop=True):
            return nc.tensor.matmul(out, lhsT, rhs, start=start, stop=stop)

        def project(L):
            w = wt[L.n]
            mm(z_ps[:, 2 * MV:ZW], zA1[:, :], w[:, W_ZA1:W_ZA2], True, False)
            mm(z_ps[:, 0:2 * MV], zA2[:, :], w[:, W_ZA2:W_ZB], False, False)
            mm(z_ps[:, 0:DV], zB[0:DV, :], w[0:DV, W_ZB:W_ZC], False, False)
            return mm(z_ps[:, DV:ZW], zC[0:DV, :], w[0:DV, W_ZC:W_END], False, True)

        def hidden_mm(L, first, rhs):
            c = W_H1 if first else W_H2
            return mm((hid1_ps if first else hid2_ps)[:, :], wt[L.n][:, c:c + P], rhs)

        def weights_mm(L, out, h, q):
            return mm(out[:, 0:384], h[:, q * P:(q + 1) * P], wt[L.n][:, W_W3:W_W3 + 384])

        def edge_pe(pe, L):
            e = es[L.n]

            def hidden1(g):
                pe.wait_ge(e["ea_in"][g.b], g.slot_count(16))
                if g.has(-1):
                    pe.wait_ge(e["h1" if L.deep else "h2"], g.times(1, 0))
                hidden_mm(L, True, ea[:, g.b, :]).then_inc(e["l1"], 1)

            def hidden2(g):
                pe.wait_ge(e["h1"], g.times(1, 1))
                if g.has(-1):
                    pe.wait_ge(e["h2"], g.times(1, 0))
                hidden_mm(L, False, h1[:, :]).then_inc(e["l2"], 1)

            def edge_weights(g, q):
                if q == 0:
                    pe.wait_ge(e["h2"], g.times(1, 1))
                if g.i is not None or g.c * PAIRS + q >= 2:
                    pe.wait_ge(e["prods"], g.times(PAIRS, q - 1))
                weights_mm(L, w_ps[q % 2], h2[:, g.b % 2, :], q).then_inc(e["w"], 1)

            def scatter(g, q):
                if q == 0:
                    pe.wait_ge(e["prep"], g.times(10, 6))
                    if g.has(-1):
                        pe.wait_ge(e["evacAB"], g.times(5, 0))
                        pe.wait_ge(e["evacC"], g.times(1, 0))
                pe.wait_ge(e["prods"], g.times(PAIRS, q + 1))
                for h in range(2):
                    t = 2 * q + h
                    o = slice(t * 4 * SLOTS, (t + 1) * 4 * SLOTS)
                    rhs = sel[:, g.b % 2, t, :, :].rearrange("p c j -> p (c j)")
                    mm(aggA_ps[:, o], prod[:, q % 2, h, 0:128], rhs)
                    mm(aggB_ps[0:DV, o], prod[:, q % 2, h, 128:224], rhs)
                    last = mm(aggC_ps[0:DV, o], prod[:, q % 2, h, 224:320], rhs)
                last.then_inc(e["scattered"], 1)

            def projection(g):
                pe.wait_ge(e["evacAB"], g.times(5, 5))
                pe.wait_ge(e["evacC"], g.times(1, 1))
                if g.has(-1):
                    pe.wait_ge(e["zsum"], g.times(1, 0))
                project(L).then_inc(e["projected"], 1)

            def combine(g):
                pe.wait_ge(e["z"], g.times(1, 1))
                mm(z_ps[:, 0:ZW], same[:, g.b % 2, :], zrow[:, :]).then_inc(e["combined"], 1)

            def body(g):
                before, after, later = G(g.i, g.c - 1), G(g.i, g.c + 1), G(g.i, g.c + 2)
                for q in range(PAIRS):
                    if q < PAIRS - 1:
                        edge_weights(g, q + 1)
                    elif g.has(1):
                        edge_weights(after, 0)
                    scatter(g, q)
                    if q == 0 and g.has(-1):
                        projection(before)
                    if q == 1:
                        if g.has(1) and L.deep:
                            hidden2(after)
                        if g.has(-1):
                            combine(before)
                    if q == PAIRS - 1 and g.has(2):
                        hidden1(later)
            hidden1(G(None, 0))
            if L.deep:
                hidden2(G(None, 0))
            hidden1(G(None, 1))
            edge_weights(G(None, 0), 0)
            groups(pe, body)
            last = G(None, GROUPS - 1)
            projection(last)
            combine(last)

        def edge_pe_general(pe, L):
            e = es[L.n]
            at, n = turns(L.deep)
            with pe.Fori(0, GROUPS) as i:
                def turn(name):
                    pe.wait_ge(e["turn"], i * n + (1 + at[name]))
                pe.wait_ge(e["loaded"][0], i * 48 + 48)
                pe.sem_inc(e["tick"], 1)
                turn("l1")
                hidden_mm(L, True, ea[:, 0, :]).then_inc(e["turn"], 1)
                if L.deep:
                    turn("l2")
                    hidden_mm(L, False, h1[:, :]).then_inc(e["turn"], 1)
                for q in range(PAIRS):
                    turn(f"w{q}")
                    weights_mm(L, w_ps[0], h2[:, 0, :], q).then_inc(e["turn"], 1)
                    for h in range(2):
                        t = 2 * q + h
                        turn(f"drow{t}")
                        nc.tensor.transpose(z_ps[:, 0:P], spread[:, :], c_(C_IDENT, P)).then_inc(e["turn"], 1)
                        turn(f"scatter{t}")
                        rhs = wide[:, :, :].rearrange("p c j -> p (c j)")
                        mm(aggA_ps[:, :], prod[:, 0, h, 0:128], rhs)
                        mm(aggB_ps[0:DV, :], prod[:, 0, h, 128:224], rhs)
                        mm(aggC_ps[0:DV, :], prod[:, 0, h, 224:320], rhs).then_inc(e["turn"], 1)
                        turn(f"project{t}")
                        project(L).then_inc(e["turn"], 1)
                        turn(f"combine{t}")
                        mm(z_ps[:, 0:ZW], same[:, 0, :], zrow[:, :]).then_inc(e["turn"], 1)

        def node_mm(l, ps, vT, sT):
            both = ps[:, 0:2 * D].rearrange("p (a n) -> p a n", a=2)
            w = wt[l]
            mm(both[:, :, 0:DV], vT, w[0:DV, W_NODEV:W_NODES].rearrange("p (a n) -> p a n", a=2), True, False)
            return mm(both[:, :, DV:D], sT, w[0:MS, W_NODES:W_H1].rearrange("p (a n) -> p a n", a=2), False, True)

        @block.tensor
        def _(pe):
            pe.wait_ge(s["consts_in"], 16)
            pe.wait_ge(s["weights_scaled"], 1)
            n0 = ns[0]

            def chunk0(i, b):
                pe.wait_ge(n0[f"in{b}"], i * 24 + 48)
                for j in range(CH):
                    tile = b * CH + j
                    if later(i) or tile >= 2:
                        pe.wait_ge(n0["made"], i * CH + (tile - 1))
                    node_mm(0, bank[3 + tile % 2], xvT[:, b, j, :], xsT[:, b, j, :]).then_inc(n0["psum"], 1)
            chunks(pe, chunk0)
            pe.wait_ge(s["span_step"], 6)
            mm(z_ps[0:1, 0:1], worst[:, 3:4], ones[:, 0:1]).then_inc(s["span_sum"], 1)
            pe.wait_ge(s["flag_set"], 1)
            choose(pe, lambda: edge_pe(pe, layers[0]), lambda: edge_pe_general(pe, layers[0]))
            n1 = ns[1]

            def chunk1(i, b):
                pe.wait_ge(n1["normed"], i + (b + 1))
                for j in range(CH + 1):
                    tile = b * CH + j
                    if j < CH:
                        if later(i) or tile >= 2:
                            pe.wait_ge(n1["turned"], i * CH + (tile - 1))
                        tp = bank[5 + tile % 2]
                        nc.tensor.transpose(tp[0:DV, 0:P], xn[:, b, j, 0:DV], c_(C_IDENT, P))
                        nc.tensor.transpose(tp[0:MS, P:2 * P], xn[:, b, j, DV:D], c_(C_IDENT, P)).then_inc(n1["transposed"], 1)
                    if j > 0:
                        tile -= 1
                        pe.wait_ge(n1["turned"], i * CH + (tile + 1))
                        if later(i) or tile >= 2:
                            pe.wait_ge(n1["made"], i * CH + (tile - 1))
                        node_mm(1, bank[3 + tile % 2], tvT[:, tile % 2, :], tsT[:, tile % 2, :]).then_inc(n1["psum"], 1)
            chunks(pe, chunk1)
            choose(pe, lambda: edge_pe(pe, layers[1]), lambda: edge_pe_general(pe, layers[1]))

        def pair_products(out, w, rows):
            w3 = w[:, 0:384].rearrange("p (h n) -> p h n", h=2)
            gs = rows[:, :, DV:D].unsqueeze(2).to_broadcast([P, 2, 2, MS])
            nc.vector.tensor_tensor(out[:, :, 0:128].rearrange("p h (k u) -> p h k u", k=2),
                                    w3[:, :, 0:128].rearrange("p h (k u) -> p h k u", k=2), gs, ALU.mult)
            for k in range(2):
                gv = rows[:, :, 0:DV].rearrange("p h (c u) -> p h c u", c=3)
                wv = w3[:, :, 128 + 32 * k:160 + 32 * k].unsqueeze(2).to_broadcast([P, 2, 3, MV])
                o = out[:, :, 128 + DV * k:128 + DV * (k + 1)].rearrange("p h (c u) -> p h c u", c=3)
                last = nc.vector.tensor_tensor(o, wv, gv, ALU.mult)
            return last

        def edge_dve(dve, L):
            e = es[L.n]

            def prods(g, q):
                if q == 0:
                    dve.wait_ge(e["gathered"][g.b], g.slot_count(16 * TILES))
                dve.wait_ge(e["w"], g.times(PAIRS, q + 1))
                if g.i is not None or g.c * PAIRS + q >= 2:
                    dve.wait_ge(e["scattered"], g.times(PAIRS, q - 1))
                pair_products(prod[:, q % 2], w_ps[q % 2], gath[:, g.b, 2 * q:2 * q + 2, :]).then_inc(e["prods"], 1)

            def evacuate(g):
                dve.wait_ge(e["scattered"], g.times(PAIRS, PAIRS))
                if g.has(-1):
                    dve.wait_ge(e["projected"], g.times(1, 0))
                evac_C(nc.vector.tensor_copy, narrow).then_inc(e["evacC"], 1)

            def step(ins):
                ins.then_inc(e["prep"], 1)

            def own(g, k):
                dve.wait_ge(e["prep"], g.times(10, k))

            def prep_ab(g):
                b, d = g.b, g.b % 2
                dve.wait_ge(e["loaded"][b], g.slot_count(32))
                if g.has(-2):
                    dve.wait_ge(e["combined"], g.times(1, -1))
                step(nc.vector.tensor_tensor(rel[:, :], ints[:, b, TILES:2 * TILES], ints[:, b, 2 * TILES:3 * TILES], ALU.subtract))
                step(nc.vector.tensor_tensor(
                    slot_row[:, :, :], ints[:, b, 2 * TILES:3 * TILES].unsqueeze(2).to_broadcast([P, TILES, SLOTS]),
                    c_(C_SLOT, SLOTS).unsqueeze(1).to_broadcast([P, TILES, SLOTS]), ALU.add))
                step(nc.vector.tensor_tensor(slot_col[:, :], ints[:, b, 3 * TILES:NI], c_(C_PMOD, 1), ALU.add))
                own(g, 1)
                step(nc.vector.tensor_tensor(
                    onehot[:, :, :], rel[:, :].unsqueeze(2).to_broadcast([P, TILES, SLOTS]),
                    c_(C_SLOT, SLOTS).unsqueeze(1).to_broadcast([P, TILES, SLOTS]), ALU.is_equal))
                own(g, 3)
                step(nc.vector.tensor_scalar(same[:, d, :], slot_row[:, :, :].rearrange("p t j -> p (t j)"),
                                             slot_col[:, 0:1], None, ALU.is_equal))

            def prep_cd(g):
                b, d = g.b, g.b % 2
                own(g, 4)
                step(nc.vector.tensor_tensor(
                    sel[:, d], onehot[:, :, :].unsqueeze(2).to_broadcast([P, TILES, 4, SLOTS]),
                    ysb[:, b].unsqueeze(3).to_broadcast([P, TILES, 4, SLOTS]), ALU.mult))
                own(g, 5)
                step(nc.vector.tensor_tensor_reduce(
                    out=earlier[:, :], in0=same[:, d, :], in1=c_(C_LOWER, P), scale=1.0, scalar=0.0,
                    op0=ALU.mult, op1=ALU.add, accum_out=dup[:, :]))
                step(nc.vector.tensor_tensor(to_trash[:, :], c_(C_TRASH, 1), slot_col[:, :], ALU.subtract))
                own(g, 7)
                step(nc.vector.tensor_scalar(is_dup[:, :], dup[:, :], 0.5, None, ALU.is_gt))
                if g.i is not None or g.c >= UNROLL:
                    dve.wait_ge(e["added"], g.times(16, -16 * (UNROLL - 1)))
                own(g, 9)
                step(nc.vector.scalar_tensor_tensor(out=target[:, b, :], in0=to_trash[:, :], scalar=is_dup[:, 0:1],
                                                    in1=slot_col[:, :], op0=ALU.mult, op1=ALU.add))

            def body(g):
                before, after = G(g.i, g.c - 1), G(g.i, g.c + 1)
                prods(g, 0)
                if g.has(-1):
                    evacuate(before)
                prods(g, 1)
                prods(g, 2)
                if g.has(1):
                    prep_ab(after)
                prods(g, 3)
                if g.has(1):
                    prep_cd(after)
            prep_ab(G(None, 0))
            prep_cd(G(None, 0))
            groups(dve, body)
            evacuate(G(None, GROUPS - 1))

        def edge_dve_general(dve, L):
            e = es[L.n]
            at, n = turns(L.deep)
            with dve.Fori(0, GROUPS) as i:
                def turn(name):
                    dve.wait_ge(e["turn"], i * n + (1 + at[name]))

                def done(ins):
                    ins.then_inc(e["turn"], 1)
                for q in range(PAIRS):
                    turn(f"prod{q}")
                    if q == 0:
                        dve.wait_ge(e["g_gathered"], i * (16 * TILES) + 16 * TILES)
                    done(pair_products(prod[:, 0], w_ps[0], gath[:, 0, 2 * q:2 * q + 2, :]))
                    for t in (2 * q, 2 * q + 1):
                        dst = ints[:, 0, TILES + t:TILES + t + 1]
                        turn(f"spread{t}")
                        done(nc.vector.tensor_copy(spread[:, :], dst.to_broadcast([P, P])))
                        turn(f"prep{t}")
                        nc.vector.tensor_copy(slot_col[:, :], dst)
                        done(nc.vector.tensor_copy(dst_row[:, :], z_ps[:, 0:P]))
                        turn(f"prep_b{t}")
                        for c in range(4):
                            nc.vector.tensor_scalar(wide[:, c, :], c_(C_IDENT, P), ysb[:, 0, t, c:c + 1], None, ALU.mult)
                        nc.vector.tensor_tensor(to_trash[:, :], c_(C_TRASH, 1), slot_col[:, :], ALU.subtract)
                        done(nc.vector.tensor_scalar(same[:, 0, :], dst_row[:, :], slot_col[:, 0:1], None, ALU.is_equal))
                        turn(f"prep_c{t}")
                        done(nc.vector.tensor_tensor_reduce(
                            out=earlier[:, :], in0=same[:, 0, :], in1=c_(C_LOWER, P), scale=1.0, scalar=0.0,
                            op0=ALU.mult, op1=ALU.add, accum_out=dup[:, :]))
                        turn(f"prep_d{t}")
                        done(nc.vector.tensor_scalar(is_dup[:, :], dup[:, :], 0.5, None, ALU.is_gt))
                        turn(f"target{t}")
                        done(nc.vector.scalar_tensor_tensor(
                            out=target[:, 0, :], in0=to_trash[:, :], scalar=is_dup[:, 0:1],
                            in1=slot_col[:, :], op0=ALU.mult, op1=ALU.add))

        def norm(dve, l, k):
            n = ns[k]
            dve.wait_ge(ns[k - 1]["base"], BASE_STEPS[k - 1] * CHUNKS)
            per = (3 if l == 0 else 1) + 3 * CH + 1

            def body(i, b):
                count = [0]

                def step(ins):
                    ins.then_inc(n["step"], 1)
                    count[0] += 1
                    return count[0]

                def own(c):
                    dve.wait_ge(n["step"], i * per + (b * per + c))
                cols = chunk_cols(i, b)
                dve.wait_ge(n[f"in{b}"], i * 8 + 16)
                if later(i):
                    if k == 1:
                        dve.wait_ge(n["base"], i + (b - 1))
                        dve.wait_ge(n["made"], i * CH + (b - 1) * CH)
                    else:
                        dve.wait_ge(n[f"out{b}"], i * 8)
                a = step(nc.vector.tensor_copy(attr[:, b, :].unsqueeze(2), base3[:, cols, D:XS]))
                factor = attr[:, b, :]
                if l == 0:
                    own(a)
                    a = step(nc.vector.tensor_tensor(gain[:, :], attr[:, b, :], attr[:, b, :], ALU.mult))
                    own(a)
                    a = step(nc.vector.tensor_tensor(gain[:, :].unsqueeze(2), gain[:, :].unsqueeze(2),
                                                     rows_in[:, b, :, D:XS], ALU.mult))
                    factor = gain
                own(a)
                us = [step(nc.vector.scalar_tensor_tensor(
                    out=resid[:, j, :], in0=rows_in[:, b, j, 0:D], scalar=factor[:, j:j + 1],
                    in1=base3[:, bass.ds((i + b) * CH + j, 1), 0:D].rearrange("p a n -> p (a n)"),
                    op0=ALU.mult, op1=ALU.add)) for j in range(CH)]
                st = []
                for j in range(CH):
                    own(us[j])
                    st.append(step(nc.vector.bn_stats(stats[:, j, :], resid[:, j, :])))
                own(st[-1])
                dve.sem_inc(s["tick"], 1)
                for j in range(CH):
                    a = step(nc.vector.bn_aggr(mv[:, j, :], stats[:, j, :]))
                own(a)
                nc.vector.tensor_scalar(std[:, :].unsqueeze(2), mv[:, :, 1:2], EPS, None, ALU.add).then_inc(n["variance"], 1)
                dve.wait_ge(n["rooted"], i + (b + 1))
                a = step(nc.vector.reciprocal(rstd[:, :], std[:, :]))
                own(a)
                for j in range(CH):
                    last = nc.vector.tensor_scalar(xn[:, b, j, :], resid[:, j, :], mv[:, j, 0:1], rstd[:, j:j + 1],
                                                   ALU.subtract, ALU.mult)
                last.then_inc(n["normed"], 1)
                assert count[0] == per
            chunks(dve, body)

        @block.vector
        def _(dve):
            nc.vector.memset(zeros[:, :], 0.0)
            nc.vector.memset(ones[:, :], 1.0)
            for l in range(2):
                nc.vector.memset(wt[l][:, :], 0.0)
            nc.vector.memset(ea[:, :, :], 0.0).then_inc(s["memsets"], 1)
            dve.wait_ge(s["dst_in"], 32)

            def link(k, ins):
                ins.then_inc(s["span_step"], 1)
                dve.wait_ge(s["span_step"], k)
            span = gath[:, 0:2, :, :].rearrange("p a t n -> p (a t n)")[:, 0:GROUPS * TILES]
            link(1, nc.vector.tensor_tensor(span, dst_all[:, :], first_all[:, :], ALU.subtract))
            link(2, nc.vector.tensor_reduce(worst[:, 0:1], span, AXX, ALU.max))
            link(3, nc.vector.tensor_reduce(worst[:, 1:2], span, AXX, ALU.min))
            link(4, nc.vector.tensor_scalar(worst[:, 2:3], worst[:, 0:1], SLOTS - 0.5, None, ALU.is_gt))
            link(5, nc.vector.tensor_scalar(worst[:, 3:4], worst[:, 1:2], -0.5, None, ALU.is_lt))
            link(6, nc.vector.tensor_tensor(worst[:, 3:4], worst[:, 3:4], worst[:, 2:3], ALU.add))
            dve.wait_ge(s["weights_in"], 16 * WEIGHT_DMAS)
            for L in layers:
                w = wt[L.n]
                own_scale = 1.0 if L.n == 0 else SIN
                for a, z, f in ((W_NODEV, W_NODEV + DV, MV ** -0.5), (W_NODEV + DV, W_NODES, MV ** -0.5 * own_scale),
                                (W_NODES, W_NODES + MS, MS ** -0.5), (W_NODES + MS, W_H1, MS ** -0.5 * own_scale),
                                (W_ZA1, W_ZC, L.kappa), (W_ZC, W_END, L.kappa * 3 ** -0.5)):
                    last = nc.vector.tensor_scalar(w[:, a:z], w[:, a:z], f, None, ALU.mult)
            last.then_inc(s["weights_scaled"], 1)
            dve.wait_ge(s["span_sum"], 1)
            nc.vector.tensor_scalar(flag[0:1, :], z_ps[0:1, 0:1], 0.5, None, ALU.is_lt).then_inc(s["flag_set"], 1)
            dve.wait_ge(s["flag_set"], 1)
            for l in range(2):
                choose(dve, lambda: edge_dve(dve, layers[l]), lambda: edge_dve_general(dve, layers[l]))
                norm(dve, l, l + 1)


def kernel(**inputs):
    import numpy as np
    import concourse.bacc as bacc
    from concourse.bass_utils import run_bass_kernel_spmd as run

    arr = {k: np.asarray(v) for k, v in inputs.items()}
    order = [1, 2, 0]
    pad = GROUPS * GROUP - N_EDGES
    x = np.pad(np.concatenate([arr["x"][:, MS:].reshape(-1, MV, 3)[:, :, order].transpose(0, 2, 1).reshape(-1, DV),
                               arr["x"][:, :MS], arr["node_vec1"]], 1), ((0, P * NT - N_NODES), (0, 0)))
    turned = x.reshape(P, NT, XS).transpose(2, 1, 0)
    src = np.pad(arr["src"], (0, pad)).reshape(GROUPS, TILES, P)
    dst = np.pad(arr["dst"], (0, pad), mode="edge").reshape(GROUPS, TILES, P)
    first = np.broadcast_to(dst[:, None, :, 0], (GROUPS, P, TILES))
    slot_first = np.repeat(dst[:, :, 0], SLOTS, 1)[:, :, None]
    ints = np.concatenate([src.transpose(0, 2, 1), dst.transpose(0, 2, 1), first, slot_first], 2)
    y = np.pad(arr["edge_attr_4"][:, [0, 2, 3, 1]], ((0, pad), (0, 0))).reshape(GROUPS, TILES, P, 4).transpose(0, 2, 1, 3)

    def hidden_in(a):
        n = a.shape[1]
        a = np.pad(a, ((0, pad), (0, 0))).reshape(GROUPS, PAIRS, 2, P, n)
        return a.transpose(0, 2, 4, 1, 3).reshape(GROUPS, 2 * n, HID)
    p = np.arange(P)
    consts = np.zeros((P, C_END), np.float32)
    consts[:, C_SLOT:C_SLOT + SLOTS] = np.arange(SLOTS)
    consts[:, C_PMOD] = p % SLOTS
    consts[:, C_TRASH] = TRASH + p
    consts[:, C_LOWER:C_LOWER + P] = p[:, None] > p[None, :]
    consts[:, C_IDENT:C_END] = np.eye(P)
    arrays = {
        "x": x, "xvT": turned[0:DV], "xsT": turned[DV:D], "ints": ints, "y": y,
        "dst_all": dst.transpose(2, 0, 1).reshape(P, -1), "first_all": first.transpose(1, 0, 2).reshape(P, -1),
        "ea8": hidden_in(arr["edge_attr_8"]), "ea16": hidden_in(arr["edge_attr_16"]), "consts": consts,
    }
    names = [dict(l1_s="Wl1_0", l1_v="Wl1_1", sc_s="Wsc0", sc_v="Wsc1", h1="Wfc1", h2="Wfc2", w3="Wfc3",
                  l2_s="Wl2_s", l2_v="Wl2_v", a="Wa"),
             dict(l1_s="W_l1_0", l1_v="W_l1_1", sc_s="W_sc0", sc_v="W_sc1", h1="fc_W1", w3="fc_W2",
                  l2_s="W_l2_0", l2_v="W_l2_1")]
    for l in range(2):
        arrays.update({f"w{l}_{k}": arr[f"L{l}_gnn_{v}"] for k, v in names[l].items()})
    nc = bacc.Bacc("TRN2", target_bir_lowering=False, num_devices=1)
    arrays = {f"in_{k}": np.ascontiguousarray(v) for k, v in arrays.items()}
    dram = {k[3:]: nc.dram_tensor(k, v.shape, mybir.dt.from_np(v.dtype), kind="ExternalInput").ap()
            for k, v in arrays.items()}
    for l in range(2):
        dram[f"w{l}"] = {k: dram[f"w{l}_{k}"] for k in names[l]}
    dram["out"] = nc.dram_tensor("out_x", (P * NT, D), F32, kind="ExternalOutput").ap()
    build(nc, dram)
    got = run(nc, [arrays], core_ids=[0]).results[0]["out_x"][:N_NODES]
    v = got[:, :DV].reshape(-1, 3, MV)[:, [2, 0, 1]].transpose(0, 2, 1).reshape(-1, DV)
    return np.concatenate([got[:, DV:], v], 1)
```

```python
from contextlib import ExitStack

import concourse.bass as bass
from concourse import mybir

F32 = mybir.dt.float32
I32 = mybir.dt.int32
ALU = mybir.AluOpType
ACT = mybir.ActivationFunctionType
AXX = mybir.AxisListType.X

P = 128
N_NODES, N_EDGES = 12500, 200000
MS, MV = 64, 32
DV, D = 3 * MV, 3 * MV + MS
DX = D - P
TILES = 8
PAIRS = TILES // 2
SLOTS = P // TILES
GROUP = TILES * P
GROUPS = -(-N_EDGES // GROUP)
UNROLL = 4
HID = GROUP // 2
WN = 2 * MS + 2 * MV
PN = 2 * P
NT = -(-N_NODES // P)
CH = 7
CHUNKS = NT // CH
ROOT_AT = CH - 3
HELPED = 4
ROWS = P * NT + P
TRASH = P * NT
ZW = D + 1
NI = 3 * TILES + 1
NB = 5
EPS = 1e-5
PREP = 6
DOTS = 3
SPAN_STEPS = 12
COS, SIN = 0.9238795325112867, 0.3826834323650898
assert GROUPS % UNROLL == 0 and NT % CH == 0 and CHUNKS % 2 == 0

W_N1 = 0
W_N2 = W_N1 + 2 * P
W_H1 = W_N2 + 2 * DX
W_H2 = W_H1 + P
W_W3 = W_H2 + P
W_ZA1 = W_W3 + 2 * WN
W_ZA2 = W_ZA1 + MV + MS + 1
W_ZB = W_ZA2 + 2 * MV
W_END = W_ZB + ZW
C_SLOT, C_PMOD, C_TRASH, C_PART, C_LOWER = 0, P, P + 1, P + 2, P + 3
C_IDENT = C_LOWER + P
C_END = C_IDENT + P


class Layer:

    def __init__(self, n, ea, attrs):
        self.n, self.ea, self.attrs = n, ea, attrs
        self.deep = n == 0
        self.func = ACT.Gelu_apprx_tanh if n == 0 else ACT.Silu
        self.scale = MS ** -0.5 * 96 ** -0.5 * (32 ** -0.5 if n == 0 else 10 ** -0.5 * COS)
        self.own_scale = 1.0 if n == 0 else SIN


class G:

    def __init__(self, j, c):
        self.j, self.c, self.b = j, c, c % UNROLL

    def plus(self, c):
        return G(self.j, self.c + c)

    def times(self, k, plus):
        return self.c * k + plus if self.j is None else self.j * (UNROLL * k) + (self.c * k + plus)

    def slot_count(self, per):
        q = self.c // UNROLL * per + per
        return q if self.j is None else self.j * per + q

    def has(self, lo):
        return self.j is not None or 0 <= self.c + lo < GROUPS

    def at(self):
        return bass.ds(self.c, 1) if self.j is None else bass.ds(self.j * UNROLL + self.c, 1)


def groups(eng, body):
    for c in range(UNROLL):
        body(G(None, c))
    with eng.Fori(1, GROUPS // UNROLL - 1) as j:
        for c in range(UNROLL):
            body(G(j, c))
    for c in range(GROUPS - UNROLL, GROUPS):
        body(G(None, c))


def chunks(eng, body):
    for b in range(2):
        body(0, b)
    with eng.Fori(1, CHUNKS // 2 - 1) as j:
        for b in range(2):
            body(j * 2, b)
    for b in range(2):
        body(CHUNKS - 2, b)


def reused(i):
    return not isinstance(i, int) or i > 0


def next_tile(i, b, j):
    if j < CH - 1:
        return i, b, j + 1
    if isinstance(i, int) and i + b == CHUNKS - 1:
        return None
    return (i, 1, 0) if b == 0 else (i + 2, 0, 0)


def chunk_cols(i, b):
    return bass.ds((i + b) * CH, CH)


def turns(deep):
    order = ["l1", "h1"] + (["l2", "h2"] if deep else []) + ["gy", "gd1", "gd2"]
    for q in range(PAIRS):
        order += [f"w{q}", f"prod{q}"]
        for t in (2 * q, 2 * q + 1):
            order += [f"{k}{t}" for k in ("spread", "drow", "prep", "prep_b", "prep_c", "prep_d", "target", "scatter",
                                          "evac", "project", "z", "combine", "zsum", "add")]
    return {n: k for k, n in enumerate(order)}, len(order)


def build(nc, dram):
    layers = [Layer(0, dram["ea8"], 8), Layer(1, dram["ea16"], 16)]
    f_dram = [nc.dram_tensor(f"f{l}", (P * NT, D), F32).ap() for l in range(2)]
    acc_dram = [nc.dram_tensor(f"acc{l}", (ROWS, ZW), F32).ap() for l in range(2)]
    x_in = dram["x"].rearrange("(p k) n -> p k n", k=NT)
    out_v = dram["out"].rearrange("(p k) n -> p k n", k=NT)
    f_v = [f.rearrange("(p k) n -> p k n", k=NT) for f in f_dram]
    acc_v = [a[0:P * NT, :].rearrange("(p k) n -> p k n", k=NT) for a in acc_dram]

    with ExitStack() as ctx:
        def sb(name, shape, dt=F32):
            return ctx.enter_context(nc.sbuf_tensor(name, shape, dt))

        def sem(name):
            return ctx.enter_context(nc.semaphore(name))

        bank = [ctx.enter_context(nc.psum_tensor(f"bank{i}", [P, 512], F32)) for i in range(8)]
        aggA_ps, aggB_ps, hid1_ps, hid2_ps, z_ps = bank[0], bank[1], bank[5], bank[6], bank[7]
        w_ps = bank[3:5]
        row_ps = bank[3:5]
        turn_ps = bank[5:7]

        consts = sb("consts", [P, C_END])
        wt = [sb(f"weights{l}", [P, W_END]) for l in range(2)]
        base = sb("base", [P, NT, D])
        attr = sb("attr", [P, NT])
        ints = sb("ints", [P, UNROLL, NI], I32)
        ysb = sb("ysb", [P, UNROLL, TILES, 4])
        ea = sb("ea", [P, UNROLL, HID])
        bases = sb("bases", [P, GROUPS + 1], I32)
        h1 = sb("h1", [P, HID])
        h2 = sb("h2", [P, 2, HID])
        gath = sb("gath", [P, UNROLL, TILES, D])
        gy = sb("gy", [P, TILES, DV])
        dots = sb("dots", [P, 2, TILES, MV])
        prod = sb("prod", [P, 2, 2, PN])
        sel = sb("sel", [P, 2, TILES, NB, SLOTS])
        rel = sb("rel", [P, TILES])
        slot_col = sb("slot_col", [P, 1])
        place = sb("place", [P, UNROLL, P])
        carry = sb("carry", [P, UNROLL, P])
        zA1, zA2, zB = (sb(n, [P, P]) for n in ("zA1", "zA2", "zB"))
        zrow = sb("zrow", [P, ZW])
        zsum = sb("zsum", [P, UNROLL, ZW])
        earlier = sb("earlier", [P, P])
        dup = sb("dup", [P, 1])
        is_dup = sb("is_dup", [P, 1])
        to_trash = sb("to_trash", [P, 1])
        target = sb("target", [P, 1], I32)
        wide = sb("wide", [P, NB, P])
        dst_row = sb("dst_row", [P, P])
        spread = sb("spread", [P, P])
        zeros = sb("zeros", [P, 3 * ZW])
        xT1 = sb("xT1", [P, 2, CH, P])
        xT2 = sb("xT2", [DX, 2, CH, P])
        rows_in = sb("rows_in", [P, 2, CH, ZW])
        two = sb("two", [P, 2, CH, 2, D])
        resid = sb("resid", [P, 2, CH, D])
        xn = sb("xn", [P, 2, CH, D])
        tT1 = sb("tT1", [P, 2, P])
        tT2 = sb("tT2", [DX, 2, P])
        gain = sb("gain", [P, CH])
        stats = sb("stats", [P, CH, 6])
        mv = sb("mv", [P, 2, CH, 2])
        std = sb("std", [P, CH])
        rstd = sb("rstd", [P, 2, CH])
        shift = sb("shift", [P, 2, CH])
        worst = sb("worst", [P, 12])
        ones = sb("ones", [P, 1])
        flag = sb("flag", [P, 1], I32)
        span = gath[:, 0:2].rearrange("p a t n -> p (a t n)")[:, 0:GROUPS * TILES]
        dst_all = gath[:, 2:4].rearrange("p a t n -> p (a t n)")[:, 0:GROUPS * TILES].bitcast(I32)
        first_all = resid[:, :].rearrange("p a t n -> p (a t n)")[:, 0:GROUPS * TILES].bitcast(I32)

        s = {n: sem(n) for n in (
            "consts_in", "bases_in", "attr_in", "memsets", "weights_in0", "weights_in1", "weights_scaled", "dst_in",
            "span_step", "span_sum", "flag_set", "tick")}
        ns = [{n: sem(f"n{k}_{n}") for n in (
            "in0", "in1", "turned_in0", "turned_in1", "transposed", "turned", "psum", "made", "base", "out0", "out1",
            "step", "variance", "rooted", "normed", "helped")} for k in range(3)]
        es = []
        for l in range(2):
            e = {n: sem(f"e{l}_{n}") for n in (
                "l1", "h1", "l2", "h2", "w", "prods", "scattered", "evac", "prep", "dots",
                "projected", "z", "combined", "zsum", "stored", "tick", "done",
                "turn", "g_gathered", "added", "acc_zeroed")}
            for n in ("loaded", "ea_in", "gathered"):
                e[n] = [sem(f"e{l}_{n}{b}") for b in range(UNROLL)]
            es.append(e)
        block = ctx.enter_context(nc.Block())

        def c_(a, n):
            return consts[:, a:a + n]

        def choose(eng, fast, general, L):
            v = eng.value_load(flag[0:1, 0:1], min_val=0, max_val=1)
            with eng.If(v):
                fast(eng, L)
            with eng.Else():
                general(eng, L)

        def load_group(sp, L, at, b, loaded, ea_in):
            sp.dma_start(ints[:, b, :], dram["ints"][at].rearrange("a p n -> (a p) n")).then_inc(loaded, 16)
            sp.dma_start(ysb[:, b], dram["y"][at].rearrange("a p t c -> (a p) t c")).then_inc(loaded, 16)
            sp.dma_start(ea[0:2 * L.attrs, b, :], L.ea[at].rearrange("a r n -> (a r) n")).then_inc(ea_in, 16)

        STORE_LAG = UNROLL + 1

        def edge_sp(sp, L):
            e = es[L.n]

            def store(g):
                row = sp.value_load(bases[0:1, g.at()], min_val=0, max_val=N_NODES)
                sp.wait_ge(e["zsum"], g.times(1, 1))
                sp.sem_inc(e["tick"], 1)
                if g.has(-1):
                    sp.wait_ge(e["stored"], g.times(16, 0))
                    sp.sem_inc(e["tick"], 1)
                sp.dma_start(acc_dram[L.n][bass.ds(row, P), :], zsum[:, g.b, :]).then_inc(e["stored"], 16)

            def body(g):
                b = g.b
                if g.has(-UNROLL):
                    sp.wait_ge(e["prods"], g.times(PAIRS, -PAIRS * (UNROLL - 1)))
                    sp.sem_inc(e["tick"], 1)
                load_group(sp, L, g.at(), b, e["loaded"][b], e["ea_in"][b])
                if g.j is not None or g.c >= STORE_LAG:
                    store(g.plus(-STORE_LAG))
            for c in range(2 * UNROLL):
                body(G(None, c))
            with sp.Fori(2, GROUPS // UNROLL) as j:
                for c in range(UNROLL):
                    body(G(j, c))
            for c in range(GROUPS - STORE_LAG, GROUPS):
                store(G(None, c))
            sp.wait_ge(e["stored"], 16 * GROUPS)

        def edge_sp_general(sp, L):
            e = es[L.n]
            _, n = turns(L.deep)
            for r in range(0, ROWS, 3 * P):
                sp.dma_start(acc_dram[L.n][r:r + 3 * P, :].rearrange("(p k) n -> p (k n)", k=3),
                             zeros[:, :]).then_inc(e["acc_zeroed"], 16)
            sp.sem_inc(e["turn"], 1)
            with sp.Fori(0, GROUPS) as i:
                sp.wait_ge(e["turn"], i * n + 1)
                sp.sem_inc(e["tick"], 1)
                load_group(sp, L, bass.ds(i, 1), 0, e["loaded"][0], e["loaded"][0])
            sp.wait_ge(e["turn"], GROUPS * n + 1)

        @block.sync
        def _(sp):
            sp.dma_start(consts[:, :], dram["consts"]).then_inc(s["consts_in"], 16)
            sp.dma_start(wt[0][:, :], dram["w0"]).then_inc(s["weights_in0"], 16)
            n0 = ns[0]

            def load0(i, b):
                if reused(i):
                    sp.wait_ge(n0["psum"], i * CH + (b - 1) * CH)
                    sp.sem_inc(s["tick"], 1)
                k = chunk_cols(i, b)
                sp.dma_start(xT1[:, b], dram["xT1"][:, k, :]).then_inc(n0[f"turned_in{b}"], 16)
                sp.dma_start(xT2[:, b], dram["xT2"][:, k, :]).then_inc(n0[f"turned_in{b}"], 16)
                if reused(i):
                    sp.wait_ge(n0["base"], i + (b - 1))
                    sp.sem_inc(s["tick"], 1)
                sp.dma_start(rows_in[:, b, :, 0:D], x_in[:, k, :]).then_inc(n0[f"in{b}"], 16)
            chunks(sp, load0)
            sp.wait_ge(s["memsets"], 1)
            sp.wait_ge(s["flag_set"], 1)
            for l in range(2):
                choose(sp, edge_sp, edge_sp_general, layers[l])
                n = ns[l + 1]
                sp.wait_ge(n0["base"], CHUNKS)

                def load(i, b):
                    if reused(i):
                        sp.wait_ge(n["variance"], i + (b - 1))
                        sp.sem_inc(s["tick"], 1)
                    sp.dma_start(rows_in[:, b], acc_v[l][:, chunk_cols(i, b), :]).then_inc(n[f"in{b}"], 16)
                chunks(sp, load)
            for b in range(2):
                sp.wait_ge(ns[2][f"out{b}"], 16 * (CHUNKS // 2))

        def gather_tile(g_out, idx, l, done):
            nc.gpsimd.indirect_dma_start(g_out, None, f_dram[l][:, :],
                                         bass.IndirectOffsetOnAxis(ap=idx, axis=0)).then_inc(done, 16)

        def edge_pool(pool, L):
            e = es[L.n]

            def body(g):
                b = g.b
                pool.wait_ge(e["loaded"][b], g.slot_count(32))
                pool.sem_inc(e["tick"], 1)
                if g.has(-UNROLL):
                    pool.wait_ge(e["prods"], g.times(PAIRS, -PAIRS * (UNROLL - 1)))
                    pool.sem_inc(e["tick"], 1)
                for t in range(TILES):
                    gather_tile(gath[:, b, t, :], ints[:, b, t:t + 1], L.n, e["gathered"][b])
            groups(pool, body)

        def edge_pool_general(pool, L):
            e = es[L.n]
            at, n = turns(L.deep)
            pool.wait_ge(e["acc_zeroed"], 16 * (ROWS // P // 3))
            with pool.Fori(0, GROUPS) as i:
                pool.wait_ge(e["loaded"][0], i * 48 + 48)
                pool.sem_inc(e["tick"], 1)
                for t in range(TILES):
                    gather_tile(gath[:, 0, t, :], ints[:, 0, t:t + 1], L.n, e["g_gathered"])
                for t in range(TILES):
                    pool.wait_ge(e["turn"], i * n + (1 + at[f"add{t}"]))
                    pool.sem_inc(e["tick"], 1)
                    nc.gpsimd.indirect_dma_start(
                        acc_dram[L.n][:, :], bass.IndirectOffsetOnAxis(ap=target[:, :], axis=0),
                        zsum[:, 0, :], None, compute_op=ALU.add).then_inc(e["added"], 16)
                    pool.wait_ge(e["added"], i * (16 * TILES) + 16 * (t + 1))
                    pool.sem_inc(e["turn"], 1)

        def base_rows(pool, k, own):
            n = ns[k]

            def body(i, b):
                if k == 0:
                    pool.wait_ge(n[f"in{b}"], i * 8 + 16)
                pool.wait_ge(n["made"], i * CH + (b + 1) * CH)
                nc.gpsimd.tensor_tensor(base[:, chunk_cols(i, b), :], two[:, b, :, 1, :], own(b),
                                        ALU.add).then_inc(n["base"], 1)
            chunks(pool, body)

        @block.gpsimd
        def _(pool):
            base_rows(pool, 0, lambda b: rows_in[:, b, :, 0:D])
            pool.wait_ge(s["flag_set"], 1)
            for l in range(2):
                if l == 1:
                    base_rows(pool, 1, lambda b: xn[:, b])
                for b in range(2):
                    pool.wait_ge(ns[l][f"out{b}"], 16 * (CHUNKS // 2))
                choose(pool, edge_pool, edge_pool_general, layers[l])
            n2 = ns[2]
            pool.wait_ge(s["attr_in"], 16)

            def help_sums(i, b):
                pool.wait_ge(n2[f"in{b}"], i * 8 + 16)
                if reused(i):
                    pool.wait_ge(n2["made"], i + (b - 1))
                last, k = slice(CH - HELPED, CH), bass.ds((i + b) * CH + (CH - HELPED), HELPED)
                nc.gpsimd.tensor_tensor(resid[:, b, last, :], rows_in[:, b, last, 0:D],
                                        attr[:, k].unsqueeze(2).to_broadcast([P, HELPED, D]), ALU.mult).then_inc(n2["helped"], 1)
                pool.wait_ge(n2["helped"], i * 2 + (2 * b + 1))
                nc.gpsimd.tensor_tensor(resid[:, b, last, :], resid[:, b, last, :], base[:, k, :],
                                        ALU.add).then_inc(n2["helped"], 1)
            chunks(pool, help_sums)

        def narrow(ps, c):
            return ps.rearrange("p (t c j) -> p t c j", c=4, j=SLOTS)[:, :, c, :]

        def broad(ps, c):
            return ps[:, c * P:(c + 1) * P]

        def evacuate(cols, done):
            for out, ps, c in ((zA1[0:64, :], aggA_ps[0:64, :], 3), (zA1[64:128, :], aggA_ps[64:128, :], 2),
                               (zA2[0:64, :], aggA_ps[64:128, :], 0), (zA2[64:128, :], aggA_ps[64:128, :], 1),
                               (zB[0:DV, :], aggB_ps[0:DV, :], 2), (zB[DV:P, :], aggB_ps[DV:P, :], 3)):
                o = out.rearrange("p (t j) -> p t j", j=SLOTS) if cols is narrow else out
                last = nc.scalar.activation(o, cols(ps, c), ACT.Copy)
            last.then_inc(done, 1)

        def activate(L, out, ps, fan_in):
            return nc.scalar.activation(out, ps[:, :], L.func, scale=fan_in ** -0.5)

        def edge_act(act, L):
            e = es[L.n]

            def hidden1(g):
                act.wait_ge(e["l1"], g.times(1, 1))
                if L.deep:
                    if g.has(-1):
                        act.wait_ge(e["l2"], g.times(1, 0))
                    activate(L, h1[:, :], hid1_ps, L.attrs).then_inc(e["h1"], 1)
                else:
                    if g.has(-2):
                        act.wait_ge(e["w"], g.times(PAIRS, -PAIRS))
                    activate(L, h2[:, g.b % 2, :], hid1_ps, L.attrs).then_inc(e["h2"], 1)

            def hidden2(g):
                act.wait_ge(e["l2"], g.times(1, 1))
                if g.has(-2):
                    act.wait_ge(e["w"], g.times(PAIRS, -PAIRS))
                activate(L, h2[:, g.b % 2, :], hid2_ps, MS).then_inc(e["h2"], 1)

            def evac(g):
                act.wait_ge(e["scattered"], g.times(PAIRS, PAIRS))
                if g.has(-1):
                    act.wait_ge(e["projected"], g.times(1, 0))
                evacuate(narrow, e["evac"])

            def zrows(g):
                act.wait_ge(e["projected"], g.times(1, 1))
                if g.has(-1):
                    act.wait_ge(e["combined"], g.times(1, 0))
                nc.scalar.activation(zrow[:, :], z_ps[:, 0:ZW], ACT.Copy).then_inc(e["z"], 1)

            def zsums(g):
                act.wait_ge(e["combined"], g.times(1, 1))
                if g.has(-UNROLL):
                    act.wait_ge(e["stored"], g.times(16, -16 * (UNROLL - 1)))
                nc.scalar.activation(zsum[:, g.b, :], z_ps[:, 0:ZW], ACT.Copy).then_inc(e["zsum"], 1)

            def body(g):
                if g.has(-1):
                    evac(g.plus(-1))
                if g.has(1):
                    hidden1(g.plus(1))
                if g.has(-1):
                    zrows(g.plus(-1))
                if g.has(1) and L.deep:
                    hidden2(g.plus(1))
                if g.has(-1):
                    zsums(g.plus(-1))
            hidden1(G(None, 0))
            if L.deep:
                hidden2(G(None, 0))
            groups(act, body)
            last = G(None, GROUPS - 1)
            evac(last)
            zrows(last)
            zsums(last)

        def edge_act_general(act, L):
            e = es[L.n]
            at, n = turns(L.deep)
            with act.Fori(0, GROUPS) as i:
                def turn(name):
                    act.wait_ge(e["turn"], i * n + (1 + at[name]))
                turn("h1")
                activate(L, h1[:, :] if L.deep else h2[:, 0, :], hid1_ps, L.attrs).then_inc(e["turn"], 1)
                if L.deep:
                    turn("h2")
                    activate(L, h2[:, 0, :], hid2_ps, MS).then_inc(e["turn"], 1)
                for t in range(TILES):
                    turn(f"evac{t}")
                    evacuate(broad, e["turn"])
                    turn(f"z{t}")
                    nc.scalar.activation(zrow[:, :], z_ps[:, 0:ZW], ACT.Copy).then_inc(e["turn"], 1)
                    turn(f"zsum{t}")
                    nc.scalar.activation(zsum[:, 0, :], z_ps[:, 0:ZW], ACT.Copy).then_inc(e["turn"], 1)

        def scaled_rows(act, k, l, before_tile):
            n = ns[k]

            def body(i, b):
                if reused(i):
                    act.wait_ge(n[f"out{b}"], i * 8)
                    act.wait_ge(n["base"], i + (b - 1))
                    act.sem_inc(s["tick"], 1)
                for j in range(CH):
                    tile = b * CH + j
                    before_tile(i, b, j)
                    act.wait_ge(n["psum"], i * CH + (tile + 1))
                    nc.scalar.activation(two[:, b, j].rearrange("p a n -> p (a n)"), row_ps[tile % 2][:, 0:2 * D],
                                         ACT.Copy, scale=attr[:, bass.ds((i + b) * CH + j, 1)]).then_inc(n["made"], 1)
                act.wait_ge(n["made"], i * CH + (b + 1) * CH)
                act.sem_inc(s["tick"], 1)
                act.dma_start(f_v[l][:, chunk_cols(i, b), :], two[:, b, :, 0, :]).then_inc(n[f"out{b}"], 16)
            return body

        def root(n, act, i, b):
            act.wait_ge(n["variance"], i + (b + 1))
            nc.scalar.activation(std[:, :], std[:, :], ACT.Sqrt).then_inc(n["rooted"], 1)

        def last_chunk(i, b):
            return isinstance(i, int) and i + b == CHUNKS - 1

        @block.scalar
        def _(act):
            act.dma_start(attr[:, :], dram["attr"]).then_inc(s["attr_in"], 16)
            act.dma_start(dst_all, dram["dst_all"]).then_inc(s["dst_in"], 16)
            act.dma_start(first_all, dram["first_all"]).then_inc(s["dst_in"], 16)
            act.dma_start(bases[:, :], dram["bases"]).then_inc(s["bases_in"], 16)
            act.dma_start(wt[1][:, :], dram["w1"]).then_inc(s["weights_in1"], 16)
            act.wait_ge(s["attr_in"], 16)
            chunks(act, scaled_rows(act, 0, 0, lambda i, b, j: None))
            act.wait_ge(s["flag_set"], 1)
            choose(act, edge_act, edge_act_general, layers[0])

            n1 = ns[1]

            def turn_over(i, b, j):
                tile = b * CH + j
                act.wait_ge(n1["transposed"], i * CH + (tile + 1))
                if reused(i) or tile >= 2:
                    act.wait_ge(n1["psum"], i * CH + (tile - 1))
                nc.scalar.activation(tT1[:, tile % 2, :], turn_ps[tile % 2][:, 0:P], ACT.Copy)
                nc.scalar.activation(tT2[:, tile % 2, :], turn_ps[tile % 2][0:DX, P:2 * P],
                                     ACT.Copy).then_inc(n1["turned"], 1)

            def turn_over_next(i, b, j):
                if j == ROOT_AT and not last_chunk(i, b):
                    root(n1, act, i, b + 1)
                after = next_tile(i, b, j)
                if after:
                    turn_over(*after)
            root(n1, act, 0, 0)
            turn_over(0, 0, 0)
            chunks(act, scaled_rows(act, 1, 1, turn_over_next))
            choose(act, edge_act, edge_act_general, layers[1])

            n2 = ns[2]

            def result(i, b):
                if reused(i):
                    act.wait_ge(n2[f"out{b}"], i * 8)
                act.wait_ge(n2["normed"], i + (b + 1))
                for j in range(CH):
                    last = nc.scalar.activation(xn[:, b, j, :], resid[:, b, j, :], ACT.Identity,
                                                bias=shift[:, b, j:j + 1], scale=rstd[:, b, j:j + 1])
                last.then_inc(n2["made"], 1)
                act.wait_ge(n2["made"], i + (b + 1))
                act.sem_inc(s["tick"], 1)
                act.dma_start(out_v[:, chunk_cols(i, b), :], xn[:, b]).then_inc(n2[f"out{b}"], 16)
                if not last_chunk(i, b):
                    root(n2, act, i, b + 1)
            root(n2, act, 0, 0)
            chunks(act, result)

        def mm(out, lhsT, rhs, start=True, stop=True):
            return nc.tensor.matmul(out, lhsT, rhs, start=start, stop=stop)

        def project(L):
            w = wt[L.n]
            mm(z_ps[:, 0:ZW], zB[:, :], w[:, W_ZB:W_END], True, False)
            mm(z_ps[:, 2 * MV:ZW], zA1[:, :], w[:, W_ZA1:W_ZA2], False, False)
            return mm(z_ps[:, 0:2 * MV], zA2[:, :], w[:, W_ZA2:W_ZB], False, True)

        def weights_mm(L, out, h, q):
            return mm(out[:, 0:2 * WN], h[:, q * P:(q + 1) * P], wt[L.n][:, W_W3:W_ZA1])

        def edge_pe(pe, L):
            e = es[L.n]

            def hidden1(g):
                pe.wait_ge(e["ea_in"][g.b], g.slot_count(16))
                if g.has(-1):
                    pe.wait_ge(e["h1" if L.deep else "h2"], g.times(1, 0))
                mm(hid1_ps[:, :], wt[L.n][:, W_H1:W_H2], ea[:, g.b, :]).then_inc(e["l1"], 1)

            def hidden2(g):
                pe.wait_ge(e["h1"], g.times(1, 1))
                if g.has(-1):
                    pe.wait_ge(e["h2"], g.times(1, 0))
                mm(hid2_ps[:, :], wt[L.n][:, W_H2:W_W3], h1[:, :]).then_inc(e["l2"], 1)

            def edge_weights(g, q):
                if q == 0:
                    pe.wait_ge(e["h2"], g.times(1, 1))
                if g.j is not None or g.c * PAIRS + q >= 2:
                    pe.wait_ge(e["prods"], g.times(PAIRS, q - 1))
                weights_mm(L, w_ps[q % 2], h2[:, g.b % 2, :], q).then_inc(e["w"], 1)

            def scatter(g, q):
                if q == 0:
                    pe.wait_ge(e["prep"], g.times(PREP, PREP))
                    if g.has(-1):
                        pe.wait_ge(e["evac"], g.times(1, 0))
                pe.wait_ge(e["prods"], g.times(PAIRS, q + 1))
                for h in range(2):
                    t = 2 * q + h
                    o = slice(t * 4 * SLOTS, (t + 1) * 4 * SLOTS)
                    blocks = sel[:, g.b % 2, t, :, :].rearrange("p c j -> p (c j)")
                    mm(aggA_ps[:, o], prod[:, q % 2, h, 0:P], blocks[:, 0:4 * SLOTS])
                    last = mm(aggB_ps[:, o], prod[:, q % 2, h, P:PN], blocks[:, SLOTS:NB * SLOTS])
                last.then_inc(e["scattered"], 1)

            def projection(g):
                pe.wait_ge(e["evac"], g.times(1, 1))
                if g.has(-1):
                    pe.wait_ge(e["zsum"], g.times(1, 0))
                project(L).then_inc(e["projected"], 1)

            def combine(g):
                pe.wait_ge(e["z"], g.times(1, 1))
                last = mm(z_ps[:, 0:ZW], place[:, g.b, :], zrow[:, :], True, not g.has(-1))
                if g.has(-1):
                    last = mm(z_ps[:, 0:ZW], carry[:, g.b, :], zsum[:, (g.b - 1) % UNROLL, :], False, True)
                last.then_inc(e["combined"], 1)

            def body(g):
                for q in range(PAIRS):
                    if q < PAIRS - 1:
                        edge_weights(g, q + 1)
                    elif g.has(1):
                        edge_weights(g.plus(1), 0)
                    scatter(g, q)
                    if q == 0 and g.has(-1):
                        projection(g.plus(-1))
                    if q == 1 and g.has(1) and L.deep:
                        hidden2(g.plus(1))
                    if q == 2 and g.has(-1):
                        combine(g.plus(-1))
                    if q == PAIRS - 1 and g.has(2):
                        hidden1(g.plus(2))
            hidden1(G(None, 0))
            if L.deep:
                hidden2(G(None, 0))
            hidden1(G(None, 1))
            edge_weights(G(None, 0), 0)
            groups(pe, body)
            last = G(None, GROUPS - 1)
            projection(last)
            combine(last)

        def edge_pe_general(pe, L):
            e = es[L.n]
            at, n = turns(L.deep)
            with pe.Fori(0, GROUPS) as i:
                def turn(name):
                    pe.wait_ge(e["turn"], i * n + (1 + at[name]))
                pe.wait_ge(e["loaded"][0], i * 48 + 48)
                pe.sem_inc(e["tick"], 1)
                turn("l1")
                mm(hid1_ps[:, :], wt[L.n][:, W_H1:W_H2], ea[:, 0, :]).then_inc(e["turn"], 1)
                if L.deep:
                    turn("l2")
                    mm(hid2_ps[:, :], wt[L.n][:, W_H2:W_W3], h1[:, :]).then_inc(e["turn"], 1)
                for q in range(PAIRS):
                    turn(f"w{q}")
                    weights_mm(L, w_ps[0], h2[:, 0, :], q).then_inc(e["turn"], 1)
                    for h in range(2):
                        t = 2 * q + h
                        turn(f"drow{t}")
                        nc.tensor.transpose(z_ps[:, 0:P], spread[:, :], c_(C_IDENT, P)).then_inc(e["turn"], 1)
                        turn(f"scatter{t}")
                        blocks = wide[:, :, :].rearrange("p c j -> p (c j)")
                        mm(aggA_ps[:, :], prod[:, 0, h, 0:P], blocks[:, 0:4 * P])
                        mm(aggB_ps[:, :], prod[:, 0, h, P:PN], blocks[:, P:NB * P]).then_inc(e["turn"], 1)
                        turn(f"project{t}")
                        project(L).then_inc(e["turn"], 1)
                        turn(f"combine{t}")
                        mm(z_ps[:, 0:ZW], place[:, 0, :], zrow[:, :]).then_inc(e["turn"], 1)

        def node_mm(l, ps, T1, T2):
            both = ps[:, 0:2 * D].rearrange("p (a n) -> p a n", a=2)
            w = wt[l]
            mm(both[:, :, DX:D], T1, w[:, W_N1:W_N2].rearrange("p (a n) -> p a n", a=2), True, False)
            return mm(both[:, :, 0:DX], T2, w[0:DX, W_N2:W_H1].rearrange("p (a n) -> p a n", a=2), False, True)

        @block.tensor
        def _(pe):
            pe.wait_ge(s["consts_in"], 16)
            pe.wait_ge(s["weights_scaled"], 1)
            n0 = ns[0]

            def chunk0(i, b):
                pe.wait_ge(n0[f"turned_in{b}"], i * 16 + 32)
                for j in range(CH):
                    tile = b * CH + j
                    if reused(i) or tile >= 2:
                        pe.wait_ge(n0["made"], i * CH + (tile - 1))
                    node_mm(0, row_ps[tile % 2], xT1[:, b, j, :], xT2[:, b, j, :]).then_inc(n0["psum"], 1)
            chunks(pe, chunk0)
            pe.wait_ge(s["span_step"], SPAN_STEPS)
            mm(z_ps[0:1, 0:1], worst[:, 11:12], ones[:, 0:1]).then_inc(s["span_sum"], 1)
            pe.wait_ge(s["flag_set"], 1)
            pe.wait_ge(s["weights_scaled"], 2)
            choose(pe, edge_pe, edge_pe_general, layers[0])
            n1 = ns[1]

            def turn_over(i, b, j):
                tile = b * CH + j
                if j == 0:
                    pe.wait_ge(n1["normed"], i + (b + 1))
                if reused(i) or tile >= 2:
                    pe.wait_ge(n1["turned"], i * CH + (tile - 1))
                tp = turn_ps[tile % 2]
                nc.tensor.transpose(tp[:, 0:P], xn[:, b, j, DX:D], c_(C_IDENT, P))
                nc.tensor.transpose(tp[0:DX, P:2 * P], xn[:, b, j, 0:DX], c_(C_IDENT, P)).then_inc(n1["transposed"], 1)

            def chunk1(i, b):
                for j in range(CH):
                    after = next_tile(i, b, j)
                    if after:
                        turn_over(*after)
                    tile = b * CH + j
                    pe.wait_ge(n1["turned"], i * CH + (tile + 1))
                    if reused(i) or tile >= 2:
                        pe.wait_ge(n1["made"], i * CH + (tile - 1))
                    node_mm(1, row_ps[tile % 2], tT1[:, tile % 2, :], tT2[:, tile % 2, :]).then_inc(n1["psum"], 1)
            turn_over(0, 0, 0)
            chunks(pe, chunk1)
            choose(pe, edge_pe, edge_pe_general, layers[1])

        def vector_times_y(rows, y):
            return nc.vector.tensor_tensor(
                gy[:, :, :].rearrange("p t (c u) -> p t c u", c=3), rows[:, :, 0:DV].rearrange("p t (c u) -> p t c u", c=3),
                y[:, :, 0:3].unsqueeze(3).to_broadcast([P, TILES, 3, MV]), ALU.mult)

        def sum_xy(out):
            return nc.vector.tensor_tensor(out, gy[:, :, 0:MV], gy[:, :, MV:2 * MV], ALU.add)

        def sum_z(out):
            return nc.vector.tensor_tensor(out, out, gy[:, :, 2 * MV:DV], ALU.add)

        def pair_products(out, w, rows, dot):
            w3 = w[:, 0:2 * WN].rearrange("p (h n) -> p h n", h=2)
            nc.vector.tensor_tensor(out[:, :, 0:P].rearrange("p h (k u) -> p h k u", k=2),
                                    w3[:, :, 0:P].rearrange("p h (k u) -> p h k u", k=2),
                                    rows[:, :, DV:D].unsqueeze(2).to_broadcast([P, 2, 2, MS]), ALU.mult)
            nc.vector.tensor_tensor(out[:, :, P:P + DV].rearrange("p h (c u) -> p h c u", c=3),
                                    w3[:, :, P:P + MV].unsqueeze(2).to_broadcast([P, 2, 3, MV]),
                                    rows[:, :, 0:DV].rearrange("p h (c u) -> p h c u", c=3), ALU.mult)
            return nc.vector.tensor_tensor(out[:, :, P + DV:PN], w3[:, :, P + MV:WN], dot, ALU.mult)

        def edge_dve(dve, L):
            e = es[L.n]

            def prods(g, q):
                if q == 0:
                    dve.wait_ge(e["dots"], g.times(DOTS, DOTS))
                dve.wait_ge(e["w"], g.times(PAIRS, q + 1))
                if g.j is not None or g.c * PAIRS + q >= 2:
                    dve.wait_ge(e["scattered"], g.times(PAIRS, q - 1))
                pair_products(prod[:, q % 2], w_ps[q % 2], gath[:, g.b, 2 * q:2 * q + 2, :],
                              dots[:, g.b % 2, 2 * q:2 * q + 2, :]).then_inc(e["prods"], 1)

            def prep(g, part):
                b, d = g.b, g.b % 2

                def step(ins):
                    ins.then_inc(e["prep"], 1)

                def own(k):
                    dve.wait_ge(e["prep"], g.times(PREP, k))
                if part == 0:
                    dve.wait_ge(e["loaded"][b], g.slot_count(32))
                    if g.has(-2):
                        dve.wait_ge(e["scattered"], g.times(PAIRS, -PAIRS))
                    if g.has(-UNROLL):
                        dve.wait_ge(e["combined"], g.times(1, -(UNROLL - 1)))
                    window, window_before = (
                        (bases[:, (g.c + k):(g.c + k) + 1] if g.j is None else bases[:, bass.ds(g.j * UNROLL + (g.c + k), 1)])
                        for k in (0, -1 if g.has(-1) else 0))
                    step(nc.vector.tensor_tensor(rel[:, :], ints[:, b, TILES:2 * TILES],
                                                 ints[:, b, 2 * TILES:3 * TILES], ALU.subtract))
                    step(nc.vector.scalar_tensor_tensor(out=slot_col[:, :], in0=ints[:, b, 3 * TILES:NI],
                                                        scalar=c_(C_PMOD, 1), in1=window, op0=ALU.add, op1=ALU.subtract))
                    step(nc.vector.scalar_tensor_tensor(out=carry[:, b, 0:1], in0=window, scalar=c_(C_PART, 1),
                                                        in1=window_before, op0=ALU.subtract, op1=ALU.is_equal))
                    own(1)
                    step(nc.vector.tensor_tensor(
                        sel[:, d, :, NB - 1, :], rel[:, :].unsqueeze(2).to_broadcast([P, TILES, SLOTS]),
                        c_(C_SLOT, SLOTS).unsqueeze(1).to_broadcast([P, TILES, SLOTS]), ALU.is_equal))
                    own(2)
                    step(nc.vector.tensor_scalar(place[:, b, :], c_(C_SLOT, P), slot_col[:, 0:1], None, ALU.is_equal))
                else:
                    own(4)
                    step(nc.vector.tensor_tensor(
                        sel[:, d, :, 0:NB - 1, :],
                        sel[:, d, :, NB - 1, :].unsqueeze(2).to_broadcast([P, TILES, NB - 1, SLOTS]),
                        ysb[:, b].unsqueeze(3).to_broadcast([P, TILES, NB - 1, SLOTS]), ALU.mult))

            def dot(g, k):
                if k == 0:
                    dve.wait_ge(e["gathered"][g.b], g.slot_count(16 * TILES))
                    vector_times_y(gath[:, g.b], ysb[:, g.b]).then_inc(e["dots"], 1)
                else:
                    dve.wait_ge(e["dots"], g.times(DOTS, k))
                    (sum_xy if k == 1 else sum_z)(dots[:, g.b % 2]).then_inc(e["dots"], 1)

            def body(g):
                after = g.plus(1)
                for q in range(PAIRS):
                    prods(g, q)
                    if g.has(1):
                        if q < 2:
                            prep(after, q)
                        else:
                            dot(after, q - 2)
                        if q == 3:
                            dot(after, 2)
            first = G(None, 0)
            prep(first, 0)
            prep(first, 1)
            for k in range(DOTS):
                dot(first, k)
            groups(dve, body)

        def edge_dve_general(dve, L):
            e = es[L.n]
            at, n = turns(L.deep)
            with dve.Fori(0, GROUPS) as i:
                def turn(name):
                    dve.wait_ge(e["turn"], i * n + (1 + at[name]))

                def done(ins):
                    ins.then_inc(e["turn"], 1)
                turn("gy")
                dve.wait_ge(e["g_gathered"], i * (16 * TILES) + 16 * TILES)
                done(vector_times_y(gath[:, 0], ysb[:, 0]))
                turn("gd1")
                done(sum_xy(dots[:, 0]))
                turn("gd2")
                done(sum_z(dots[:, 0]))
                for q in range(PAIRS):
                    turn(f"prod{q}")
                    done(pair_products(prod[:, 0], w_ps[0], gath[:, 0, 2 * q:2 * q + 2, :], dots[:, 0, 2 * q:2 * q + 2, :]))
                    for t in (2 * q, 2 * q + 1):
                        dst = ints[:, 0, TILES + t:TILES + t + 1]
                        turn(f"spread{t}")
                        done(nc.vector.tensor_copy(spread[:, :], dst.to_broadcast([P, P])))
                        turn(f"prep{t}")
                        nc.vector.tensor_copy(slot_col[:, :], dst)
                        done(nc.vector.tensor_copy(dst_row[:, :], z_ps[:, 0:P]))
                        turn(f"prep_b{t}")
                        for c in range(4):
                            nc.vector.tensor_scalar(wide[:, c, :], c_(C_IDENT, P), ysb[:, 0, t, c:c + 1], None, ALU.mult)
                        nc.vector.tensor_copy(wide[:, 4, :], c_(C_IDENT, P))
                        nc.vector.tensor_tensor(to_trash[:, :], c_(C_TRASH, 1), slot_col[:, :], ALU.subtract)
                        done(nc.vector.tensor_scalar(place[:, 0, :], dst_row[:, :], slot_col[:, 0:1], None, ALU.is_equal))
                        turn(f"prep_c{t}")
                        done(nc.vector.tensor_tensor_reduce(
                            out=earlier[:, :], in0=place[:, 0, :], in1=c_(C_LOWER, P), scale=1.0, scalar=0.0,
                            op0=ALU.mult, op1=ALU.add, accum_out=dup[:, :]))
                        turn(f"prep_d{t}")
                        done(nc.vector.tensor_scalar(is_dup[:, :], dup[:, :], 0.5, None, ALU.is_gt))
                        turn(f"target{t}")
                        done(nc.vector.scalar_tensor_tensor(
                            out=target[:, :], in0=to_trash[:, :], scalar=is_dup[:, 0:1],
                            in1=slot_col[:, :], op0=ALU.mult, op1=ALU.add))

        def norm(dve, l):
            k = l + 1
            n = ns[k]
            own_sums = CH if l == 0 else CH - HELPED
            per = (2 if l == 0 else 1) + own_sums + CH + 2
            dve.wait_ge(ns[k - 1]["base"], CHUNKS)
            dve.wait_ge(s["attr_in"], 16)

            def body(i, b):
                count = [0]

                def step(ins):
                    ins.then_inc(n["step"], 1)
                    count[0] += 1
                    return count[0]

                def own(c):
                    dve.wait_ge(n["step"], i * per + (b * per + c))
                dve.wait_ge(n[f"in{b}"], i * 8 + 16)
                if reused(i) and k == 2:
                    dve.wait_ge(n["made"], i + (b - 1))
                a_cols = attr[:, chunk_cols(i, b)]
                if l == 0:
                    own(step(nc.vector.tensor_tensor(gain[:, :], a_cols, a_cols, ALU.mult)))
                    a = step(nc.vector.tensor_tensor(gain[:, :].unsqueeze(2), gain[:, :].unsqueeze(2),
                                                     rows_in[:, b, :, D:ZW], ALU.mult))
                else:
                    a = step(nc.vector.tensor_copy(gain[:, :], a_cols))
                own(a)
                us = [step(nc.vector.scalar_tensor_tensor(
                    out=resid[:, b, j, :], in0=rows_in[:, b, j, 0:D], scalar=gain[:, j:j + 1],
                    in1=base[:, bass.ds((i + b) * CH + j, 1), :].rearrange("p a n -> p (a n)"),
                    op0=ALU.mult, op1=ALU.add)) for j in range(own_sums)]
                for j in range(CH):
                    if j < own_sums:
                        own(us[j])
                    elif j == own_sums:
                        dve.wait_ge(n["helped"], i * 2 + (2 * b + 2))
                    a = step(nc.vector.bn_stats(stats[:, j, :], resid[:, b, j, :]))
                own(a)
                dve.sem_inc(s["tick"], 1)
                for j in range(CH):
                    last = nc.vector.bn_aggr(mv[:, b, j, :], stats[:, j, :])
                own(step(last))
                nc.vector.tensor_scalar(std[:, :].unsqueeze(2), mv[:, b, :, 1:2], EPS, None, ALU.add).then_inc(n["variance"], 1)
                dve.wait_ge(n["rooted"], i + (b + 1))
                own(step(nc.vector.reciprocal(rstd[:, b, :], std[:, :])))
                if k == 1:
                    if reused(i):
                        dve.wait_ge(n["base"], i + (b - 1))
                    for j in range(CH):
                        last = nc.vector.tensor_scalar(xn[:, b, j, :], resid[:, b, j, :], mv[:, b, j, 0:1],
                                                       rstd[:, b, j:j + 1], ALU.subtract, ALU.mult)
                else:
                    last = nc.vector.scalar_tensor_tensor(out=shift[:, b, :].unsqueeze(2), in0=mv[:, b, :, 0:1], scalar=-1.0,
                                                          in1=rstd[:, b, :].unsqueeze(2), op0=ALU.mult, op1=ALU.mult)
                last.then_inc(n["normed"], 1)
                assert count[0] == per
            chunks(dve, body)

        def look_at_dst(dve):
            count = [0]

            def link(ins):
                count[0] += 1
                ins.then_inc(s["span_step"], 1)
                dve.wait_ge(s["span_step"], count[0])

            def per_group(ap):
                return ap.rearrange("p (g t) -> p g t", t=TILES)

            def of_groups(lo):
                return bases[:, lo:lo + GROUPS].unsqueeze(2).to_broadcast([P, GROUPS, TILES])

            def extreme(k, ap, op):
                return nc.vector.tensor_reduce(worst[:, k:k + 1], ap, AXX, op)
            dve.wait_ge(s["dst_in"], 32)
            dve.wait_ge(s["bases_in"], 16)
            link(nc.vector.tensor_tensor(span, dst_all, first_all, ALU.subtract))
            extreme(0, span, ALU.max)
            link(extreme(1, span, ALU.min))
            link(nc.vector.tensor_tensor(per_group(span), per_group(dst_all), of_groups(1), ALU.subtract))
            link(extreme(2, span, ALU.max))
            link(nc.vector.tensor_tensor(per_group(span), per_group(dst_all), of_groups(0), ALU.subtract))
            link(extreme(3, span, ALU.min))
            link(nc.vector.tensor_tensor(span[:, 0:GROUPS], bases[:, 1:GROUPS + 1], bases[:, 0:GROUPS], ALU.subtract))
            link(extreme(4, span[:, 0:GROUPS], ALU.max))
            for a, lim, op in ((0, SLOTS - 0.5, ALU.is_gt), (1, -0.5, ALU.is_lt), (2, 0.5, ALU.is_gt),
                               (3, -0.5, ALU.is_lt)):
                nc.vector.tensor_scalar(worst[:, 5 + a:6 + a], worst[:, a:a + 1], lim, None, op)
            link(nc.vector.tensor_scalar(worst[:, 9:10], worst[:, 4:5], P - 0.5, None, ALU.is_gt))
            link(nc.vector.tensor_tensor(worst[:, 5:7], worst[:, 5:7], worst[:, 7:9], ALU.add))
            link(nc.vector.tensor_tensor(worst[:, 10:11], worst[:, 5:6], worst[:, 6:7], ALU.add))
            link(nc.vector.tensor_tensor(worst[:, 11:12], worst[:, 10:11], worst[:, 9:10], ALU.add))
            assert count[0] == SPAN_STEPS

        @block.vector
        def _(dve):
            for L in layers:
                dve.wait_ge(s[f"weights_in{L.n}"], 16)
                w, own_s, own_v = wt[L.n], MS ** -0.5, MV ** -0.5
                for f, c in ((1.0, 0), (L.own_scale, 1)):
                    a = W_N1 + c * P
                    nc.vector.tensor_scalar(w[:, a:a + 2 * MV], w[:, a:a + 2 * MV], own_v * f, None, ALU.mult)
                    nc.vector.tensor_scalar(w[:, a + 2 * MV:a + P], w[:, a + 2 * MV:a + P], own_s * f, None, ALU.mult)
                    a = W_N2 + c * DX
                    last = nc.vector.tensor_scalar(w[:, a:a + DX], w[:, a:a + DX], own_v * f, None, ALU.mult)
                if L.n == 0:
                    last.then_inc(s["weights_scaled"], 1)
                nc.vector.tensor_scalar(w[:, W_ZA1:W_ZB], w[:, W_ZA1:W_ZB], L.scale, None, ALU.mult)
                nc.vector.tensor_scalar(w[0:DV, W_ZB:W_END], w[0:DV, W_ZB:W_END], L.scale, None, ALU.mult)
                last = nc.vector.tensor_scalar(w[DV:P, W_ZB:W_END], w[DV:P, W_ZB:W_END], L.scale * 3 ** -0.5, None, ALU.mult)
            last.then_inc(s["weights_scaled"], 1)
            nc.vector.memset(zeros[:, :], 0.0)
            nc.vector.memset(ones[:, :], 1.0)
            nc.vector.memset(carry[:, :, :], 0.0)
            nc.vector.memset(ea[:, :, :], 0.0).then_inc(s["memsets"], 1)
            dve.wait_ge(s["consts_in"], 16)
            look_at_dst(dve)
            dve.wait_ge(s["span_sum"], 1)
            nc.vector.tensor_scalar(flag[0:1, :], z_ps[0:1, 0:1], 0.5, None, ALU.is_lt).then_inc(s["flag_set"], 1)
            dve.wait_ge(s["flag_set"], 1)
            for l in range(2):
                choose(dve, edge_dve, edge_dve_general, layers[l])
                norm(dve, l)


def kernel(**inputs):
    import numpy as np
    import concourse.bacc as bacc
    from concourse.bass_utils import run_bass_kernel_spmd as run

    arr = {k: np.asarray(v) for k, v in inputs.items()}
    pad = GROUPS * GROUP - N_EDGES
    x = np.pad(np.concatenate([arr["x"][:, MS:].reshape(-1, MV, 3).transpose(0, 2, 1).reshape(-1, DV),
                               arr["x"][:, :MS]], 1), ((0, P * NT - N_NODES), (0, 0)))
    attr = np.pad(arr["node_vec1"], ((0, P * NT - N_NODES), (0, 0))).reshape(P, NT)
    turned = x.reshape(P, NT, D).transpose(2, 1, 0)
    src = np.pad(arr["src"], (0, pad)).reshape(GROUPS, TILES, P)
    dst = np.pad(arr["dst"], (0, pad), mode="edge").reshape(GROUPS, TILES, P)
    first = np.broadcast_to(dst[:, None, :, 0], (GROUPS, P, TILES))
    slot_first = np.repeat(dst[:, :, 0], SLOTS, 1)[:, :, None]
    ints = np.concatenate([src.transpose(0, 2, 1), dst.transpose(0, 2, 1), first, slot_first], 2)
    ends = np.zeros(1, dst.dtype), np.full(1, N_NODES, dst.dtype)
    bases = np.broadcast_to(np.concatenate([ends[0], dst[1:, 0, 0], ends[1]]), (P, GROUPS + 1))
    y = np.pad(arr["edge_attr_4"][:, [1, 2, 3, 0]], ((0, pad), (0, 0))).reshape(GROUPS, TILES, P, 4).transpose(0, 2, 1, 3)

    def hidden_in(a):
        n = a.shape[1]
        a = np.pad(a, ((0, pad), (0, 0))).reshape(GROUPS, PAIRS, 2, P, n)
        return a.transpose(0, 2, 4, 1, 3).reshape(GROUPS, 2 * n, HID)
    p = np.arange(P)
    consts = np.zeros((P, C_END), np.float32)
    consts[:, C_SLOT:C_SLOT + P] = p
    consts[:, C_PMOD] = p % SLOTS
    consts[:, C_TRASH] = TRASH + p
    consts[:, C_PART] = p
    consts[:, C_LOWER:C_LOWER + P] = p[:, None] > p[None, :]
    consts[:, C_IDENT:C_END] = np.eye(P)

    def weights(l, l1_s, l1_v, sc_s, sc_v, h, w3, l2_s, l2_v, a):
        w = np.zeros((P, W_END), arr["x"].dtype)

        def put(r, c, block):
            w[r:r + block.shape[0], c:c + block.shape[1]] = block
        for k, (ws, wv) in enumerate(((l1_s, l1_v), (sc_s, sc_v))):
            for v in range(2):
                put(MV * v, W_N1 + k * P + MV * v, wv)
            put(2 * MV, W_N1 + k * P + 2 * MV, ws)
            put(0, W_N2 + k * DX, wv)
        for half in range(2):
            put(h[0].shape[0] * half, W_H1 + MS * half, h[0])
            if len(h) > 1:
                put(MS * half, W_H2 + MS * half, h[1])
            put(MS * half, W_W3 + WN * half, w3)
            put(MS * half, W_ZA2 + MV * half, l2_v[:MS])
        put(MS, W_ZA1, l2_v[:MS])
        put(0, W_ZA1 + MV, l2_s[:MS])
        for v in range(3):
            put(MV * v, W_ZB + MV * v, l2_v[MS:])
        put(DV, W_ZB + DV, l2_s[MS:])
        if a is not None:
            put(0, W_ZA1 + MV + MS, a[:MS])
            put(DV, W_ZB + D, a[MS:])
        return w
    g = lambda l, n: arr[f"L{l}_gnn_{n}"]
    arrays = {
        "x": x, "attr": attr, "xT1": turned[DX:D], "xT2": turned[0:DX], "ints": ints, "y": y, "bases": bases,
        "dst_all": dst.transpose(2, 0, 1).reshape(P, -1), "first_all": first.transpose(1, 0, 2).reshape(P, -1),
        "ea8": hidden_in(arr["edge_attr_8"]), "ea16": hidden_in(arr["edge_attr_16"]), "consts": consts,
        "w0": weights(0, g(0, "Wl1_0"), g(0, "Wl1_1"), g(0, "Wsc0"), g(0, "Wsc1"), [g(0, "Wfc1"), g(0, "Wfc2")],
                      g(0, "Wfc3"), g(0, "Wl2_s"), g(0, "Wl2_v"), g(0, "Wa")),
        "w1": weights(1, g(1, "W_l1_0"), g(1, "W_l1_1"), g(1, "W_sc0"), g(1, "W_sc1"), [g(1, "fc_W1")],
                      g(1, "fc_W2"), g(1, "W_l2_0"), g(1, "W_l2_1"), None),
    }
    nc = bacc.Bacc("TRN2", target_bir_lowering=False, num_devices=1)
    arrays = {f"in_{k}": np.ascontiguousarray(v) for k, v in arrays.items()}
    dram = {k[3:]: nc.dram_tensor(k, v.shape, mybir.dt.from_np(v.dtype), kind="ExternalInput").ap()
            for k, v in arrays.items()}
    dram["out"] = nc.dram_tensor("out_x", (P * NT, D), F32, kind="ExternalOutput").ap()
    build(nc, dram)
    got = run(nc, [arrays], core_ids=[0]).results[0]["out_x"][:N_NODES]
    return np.concatenate([got[:, DV:], got[:, :DV].reshape(-1, 3, MV).transpose(0, 2, 1).reshape(-1, DV)], 1)
```

```python
from contextlib import ExitStack

import concourse.bass as bass
from concourse import mybir

F32 = mybir.dt.float32
BF16 = mybir.dt.bfloat16
I32 = mybir.dt.int32
ALU = mybir.AluOpType
ACT = mybir.ActivationFunctionType
AXX = mybir.AxisListType.X

P = 128
N_NODES, N_EDGES = 12500, 200000
MS, MV = 64, 32
DV, D = 3 * MV, 3 * MV + MS
DX = D - P
TILES = 8
PAIRS = TILES // 2
SLOTS = P // TILES
GROUP = TILES * P
GROUPS = -(-N_EDGES // GROUP)
UNROLL = 4
HID = GROUP // 2
WN = 2 * MS + 2 * MV
PN = 2 * P
NT = -(-N_NODES // P)
CH = 7
CHUNKS = NT // CH
QUAD = 4
QUADS = -(-CH // QUAD)
PIECE = GROUPS * GROUP * 8 // P // CHUNKS
W_PARTS = (0, 0, 0, 1, 1, 1, 2, 2)
HELPED = 4
ROWS = P * NT + P
TRASH = P * NT
ZW = D + 1
NI = 3 * TILES + 1
NB = 5
EPS = 1e-5
PREP = 6
DOTS = 3
SPAN_STEPS = 12
COS, SIN = 0.9238795325112867, 0.3826834323650898
assert GROUPS % UNROLL == 0 and NT % CH == 0 and CHUNKS % 2 == 0

W_N1 = 0
W_N2 = W_N1 + 2 * P
W_H1 = W_N2 + QUAD * 2 * DX
W_H2 = W_H1 + P
W_W3 = W_H2 + P
W_ZA1 = W_W3 + 2 * WN
W_ZA2 = W_ZA1 + MV + MS + 1
W_ZB = W_ZA2 + 2 * MV
W_END = W_ZB + ZW
C_SLOT, C_PMOD, C_TRASH, C_PART, C_LOWER = 0, P, P + 1, P + 2, P + 3
C_IDENT = C_LOWER + P
C_MASK = C_IDENT + P
C_END = C_MASK + 3


class Layer:

    def __init__(self, n, ea, attrs):
        self.n, self.ea, self.attrs = n, ea, attrs
        self.deep = n == 0
        self.ea_counts = 48 if n == 0 else 16
        self.func = ACT.Gelu_apprx_tanh if n == 0 else ACT.Silu
        self.scale = MS ** -0.5 * 96 ** -0.5 * (32 ** -0.5 if n == 0 else 10 ** -0.5 * COS)
        self.own_scale = 1.0 if n == 0 else SIN


class G:

    def __init__(self, j, c):
        self.j, self.c, self.b = j, c, c % UNROLL

    def plus(self, c):
        return G(self.j, self.c + c)

    def times(self, k, plus):
        return self.c * k + plus if self.j is None else self.j * (UNROLL * k) + (self.c * k + plus)

    def slot_count(self, per):
        q = self.c // UNROLL * per + per
        return q if self.j is None else self.j * per + q

    def has(self, lo):
        return self.j is not None or 0 <= self.c + lo < GROUPS

    def at(self):
        return bass.ds(self.c, 1) if self.j is None else bass.ds(self.j * UNROLL + self.c, 1)


def groups(eng, body):
    for c in range(UNROLL):
        body(G(None, c))
    with eng.Fori(1, GROUPS // UNROLL - 1) as j:
        for c in range(UNROLL):
            body(G(j, c))
    for c in range(GROUPS - UNROLL, GROUPS):
        body(G(None, c))


def chunks(eng, body):
    for b in range(2):
        body(0, b)
    with eng.Fori(1, CHUNKS // 2 - 1) as j:
        for b in range(2):
            body(j * 2, b)
    for b in range(2):
        body(CHUNKS - 2, b)


def reused(i):
    return not isinstance(i, int) or i > 0


def next_chunk(i, b):
    if isinstance(i, int) and i + b == CHUNKS - 1:
        return None
    return (i, 1) if b == 0 else (i + 2, 0)


def next_tile(i, b, j):
    if j < CH - 1:
        return i, b, j + 1
    after = next_chunk(i, b)
    return after and (*after, 0)


def chunk_cols(i, b):
    return bass.ds((i + b) * CH, CH)


def turns(deep):
    order = ["l1", "h1"] + (["l2", "h2"] if deep else []) + ["gy", "gd1", "gd2"]
    for q in range(PAIRS):
        order += [f"w{q}", f"prod{q}"]
        for t in (2 * q, 2 * q + 1):
            order += [f"{k}{t}" for k in ("spread", "drow", "prep", "prep_b", "prep_c", "prep_d", "target", "scatter",
                                          "evac", "project", "z", "combine", "zsum", "add")]
    return {n: k for k, n in enumerate(order)}, len(order)


def build(nc, dram):
    layers = [Layer(0, dram["ea8"], 8), Layer(1, dram["ea16"], 16)]
    f_dram = [nc.dram_tensor(f"f{l}", (P * NT, D), F32).ap() for l in range(2)]
    acc_dram = [nc.dram_tensor(f"acc{l}", (ROWS, ZW), F32).ap() for l in range(2)]
    parts_dram = nc.dram_tensor("parts", (3, GROUPS, 2 * layers[0].attrs, HID), BF16).ap()
    parts_v = parts_dram.rearrange("a g r n -> a (g r n)").rearrange("a (p n) -> p a n", p=P)
    ea8_v = dram["ea8"].rearrange("g r n -> (g r n)").rearrange("(p n) -> p n", p=P)
    x_in = dram["x"].rearrange("(p k) n -> p k n", k=NT)
    out_v = dram["out"].rearrange("(p k) n -> p k n", k=NT)
    f_v = [f.rearrange("(p k) n -> p k n", k=NT) for f in f_dram]
    acc_v = [a[0:P * NT, :].rearrange("(p k) n -> p k n", k=NT) for a in acc_dram]

    with ExitStack() as ctx:
        def sb(name, shape, dt=F32):
            return ctx.enter_context(nc.sbuf_tensor(name, shape, dt))

        def sem(name):
            return ctx.enter_context(nc.semaphore(name))

        bank = [ctx.enter_context(nc.psum_tensor(f"bank{i}", [P, 512], F32)) for i in range(8)]
        aggA_ps = [bank[0], bank[2]]
        aggB_ps, hid1_ps, hid2_ps, z_ps = bank[1], bank[5], bank[6], bank[7]
        w_ps = bank[3:5]
        row_ps, quad_ps, turn_ps, turn_quad_ps = bank[3:5], [bank[0], bank[2]], bank[5:7], [bank[1], bank[7]]

        consts = sb("consts", [P, C_END])
        wt = [sb(f"weights{l}", [P, W_END]) for l in range(2)]
        base = sb("base", [P, NT, D])
        attr = sb("attr", [P, NT])
        ints = sb("ints", [P, UNROLL, NI], I32)
        ysb = sb("ysb", [P, UNROLL, TILES, 4])
        ea = sb("ea", [P, UNROLL, HID])
        ea_parts = sb("ea_parts", [P, UNROLL, HID], BF16)
        wh1 = sb("wh1", [P, P], BF16)
        bases = sb("bases", [P, GROUPS + 1], I32)
        h1 = sb("h1", [P, HID])
        h2 = sb("h2", [P, 2, HID])
        gath = sb("gath", [P, UNROLL, TILES, D])
        gy = sb("gy", [P, TILES, DV])
        dots = sb("dots", [P, 2, TILES, MV])
        prod = sb("prod", [P, 2, 2, PN])
        sel = sb("sel", [P, 2, TILES, NB, SLOTS])
        rel = sb("rel", [P, TILES])
        slot_col = sb("slot_col", [P, 1])
        place = sb("place", [P, UNROLL, P])
        carry = sb("carry", [P, UNROLL, P])
        zA1, zA2, zB = (sb(n, [P, P]) for n in ("zA1", "zA2", "zB"))
        zrow = sb("zrow", [P, ZW])
        zsum = sb("zsum", [P, UNROLL, ZW])
        earlier = sb("earlier", [P, P])
        dup = sb("dup", [P, 1])
        is_dup = sb("is_dup", [P, 1])
        to_trash = sb("to_trash", [P, 1])
        target = sb("target", [P, 1], I32)
        wide = sb("wide", [P, NB, P])
        dst_row = sb("dst_row", [P, P])
        spread = sb("spread", [P, P])
        zeros = sb("zeros", [P, 3 * ZW])
        xT1 = sb("xT1", [P, 2, CH, P])
        xT2 = sb("xT2", [P, 2, QUADS, P])
        rows_in = sb("rows_in", [P, 2, CH, ZW])
        two = sb("two", [P, 2, CH, 2, D])
        resid = sb("resid", [P, 2, CH, D])
        xn = sb("xn", [P, 2, CH, D])
        vx = sb("vx", [P, 2, CH * DX])
        tT1 = sb("tT1", [P, 2, P])
        tT2 = sb("tT2", [P, QUADS, P])
        gain = sb("gain", [P, CH])
        stats = sb("stats", [P, CH, 6])
        mv = sb("mv", [P, 2, CH, 2])
        std = sb("std", [P, 2, CH])
        rstd = sb("rstd", [P, 2, CH])
        shift = sb("shift", [P, 2, CH])
        piece_in = xn[:, :].rearrange("p a t n -> p (a t n)")[:, 0:2 * PIECE].rearrange("p (b n) -> p b n", b=2)
        rest = prod[:, :].rearrange("p a h n -> p (a h n)")[:, 0:PIECE]
        piece_parts = gath[:, :].rearrange("p a t n -> p (a t n)").bitcast(BF16)[:, 0:6 * PIECE].rearrange(
            "p (b k n) -> p b k n", b=2, k=3)
        w_parts = sb("w_parts", [P, 3, P], BF16)
        w_rest = sb("w_rest", [P, 2, P])
        w_sum = sb("w_sum", [P, 2, P], BF16)
        worst = sb("worst", [P, 12])
        ones = sb("ones", [P, 1])
        flag = sb("flag", [P, 1], I32)
        span = gath[:, 0:2].rearrange("p a t n -> p (a t n)")[:, 0:GROUPS * TILES]
        dst_all = gath[:, 2:4].rearrange("p a t n -> p (a t n)")[:, 0:GROUPS * TILES].bitcast(I32)
        first_all = resid[:, :].rearrange("p a t n -> p (a t n)")[:, 0:GROUPS * TILES].bitcast(I32)

        s = {n: sem(n) for n in (
            "consts_in", "bases_in", "attr_in", "memsets", "weights_in0", "weights_in1", "weights_scaled", "dst_in",
            "span_step", "span_sum", "flag_set", "tick", "w_split_step", "split_step", "split", "piece_in0", "piece_in1",
            "parts_out0", "parts_out1")}
        ns = [{n: sem(f"n{k}_{n}") for n in (
            "in0", "in1", "turned_in0", "turned_in1", "transposed", "turned", "psum", "made", "base", "out0", "out1",
            "step", "variance", "rooted", "inverted", "normed", "packed", "helped")} for k in range(3)]
        es = []
        for l in range(2):
            e = {n: sem(f"e{l}_{n}") for n in (
                "l1", "h1", "l2", "h2", "w", "prods", "scattered", "evac_b", "evac", "prep", "dots",
                "projected", "z", "combined", "zsum", "stored", "tick", "done",
                "turn", "g_gathered", "added", "acc_zeroed")}
            for n in ("loaded", "ea_in", "gathered"):
                e[n] = [sem(f"e{l}_{n}{b}") for b in range(UNROLL)]
            es.append(e)
        block = ctx.enter_context(nc.Block())

        def c_(a, n):
            return consts[:, a:a + n]

        def choose(eng, fast, general, L):
            v = eng.value_load(flag[0:1, 0:1], min_val=0, max_val=1)
            with eng.If(v):
                fast(eng, L)
            with eng.Else():
                general(eng, L)

        def load_group(sp, L, at, b, loaded, ea_in):
            sp.dma_start(ints[:, b, :], dram["ints"][at].rearrange("a p n -> (a p) n")).then_inc(loaded, 16)
            sp.dma_start(ysb[:, b], dram["y"][at].rearrange("a p t c -> (a p) t c")).then_inc(loaded, 16)
            if L.deep:
                for lo, n in ((0, 3), (3, 3), (6, 2)):
                    rows = slice(lo * 2 * L.attrs, (lo + n) * 2 * L.attrs)
                    sp.dma_start(ea_parts[rows, b, :],
                                 parts_dram[0:n, at].rearrange("a g r n -> a (g r) n")).then_inc(ea_in, 16)
            else:
                sp.dma_start(ea[0:2 * L.attrs, b, :], L.ea[at].rearrange("a r n -> (a r) n")).then_inc(ea_in, 16)

        STORE_LAG = UNROLL + 1

        def edge_sp(sp, L):
            e = es[L.n]

            def store(g):
                row = sp.value_load(bases[0:1, g.at()], min_val=0, max_val=N_NODES)
                sp.wait_ge(e["zsum"], g.times(1, 1))
                sp.sem_inc(e["tick"], 1)
                if g.has(-1):
                    sp.wait_ge(e["stored"], g.times(16, 0))
                    sp.sem_inc(e["tick"], 1)
                sp.dma_start(acc_dram[L.n][bass.ds(row, P), :], zsum[:, g.b, :]).then_inc(e["stored"], 16)

            def body(g):
                b = g.b
                if g.has(-UNROLL):
                    sp.wait_ge(e["prods"], g.times(PAIRS, -PAIRS * (UNROLL - 1)))
                    sp.sem_inc(e["tick"], 1)
                load_group(sp, L, g.at(), b, e["loaded"][b], e["ea_in"][b])
                if g.j is not None or g.c >= STORE_LAG:
                    store(g.plus(-STORE_LAG))
            for c in range(2 * UNROLL):
                body(G(None, c))
            with sp.Fori(2, GROUPS // UNROLL) as j:
                for c in range(UNROLL):
                    body(G(j, c))
            for c in range(GROUPS - STORE_LAG, GROUPS):
                store(G(None, c))
            sp.wait_ge(e["stored"], 16 * GROUPS)

        def edge_sp_general(sp, L):
            e = es[L.n]
            _, n = turns(L.deep)
            for r in range(0, ROWS, 3 * P):
                sp.dma_start(acc_dram[L.n][r:r + 3 * P, :].rearrange("(p k) n -> p (k n)", k=3),
                             zeros[:, :]).then_inc(e["acc_zeroed"], 16)
            sp.sem_inc(e["turn"], 1)
            with sp.Fori(0, GROUPS) as i:
                sp.wait_ge(e["turn"], i * n + 1)
                sp.sem_inc(e["tick"], 1)
                load_group(sp, L, bass.ds(i, 1), 0, e["loaded"][0], e["loaded"][0])
            sp.wait_ge(e["turn"], GROUPS * n + 1)

        @block.sync
        def _(sp):
            sp.dma_start(consts[:, :], dram["consts"]).then_inc(s["consts_in"], 16)
            sp.dma_start(wt[0][:, :], dram["w0"]).then_inc(s["weights_in0"], 16)
            n0 = ns[0]

            def load0(i, b):
                if reused(i):
                    sp.wait_ge(n0["psum"], i * CH + (b - 1) * CH)
                    sp.sem_inc(s["tick"], 1)
                k = chunk_cols(i, b)
                sp.dma_start(xT1[:, b], dram["xT1"][:, k, :]).then_inc(n0[f"turned_in{b}"], 16)
                sp.dma_start(xT2[:, b], dram["xT2"][:, bass.ds((i + b) * QUADS, QUADS), :]).then_inc(n0[f"turned_in{b}"], 16)
                if reused(i):
                    sp.wait_ge(n0["base"], i + (b - 1))
                    sp.sem_inc(s["tick"], 1)
                sp.dma_start(rows_in[:, b, :, 0:D], x_in[:, k, :]).then_inc(n0[f"in{b}"], 16)

            def load_piece(i, b):
                sp.dma_start(piece_in[:, b], ea8_v[:, bass.ds((i + b) * PIECE, PIECE)]).then_inc(s[f"piece_in{b}"], 16)

            def store_parts(i, b):
                sp.wait_ge(s["split"], i + (b + 1))
                sp.sem_inc(s["tick"], 1)
                sp.dma_start(parts_v[:, :, bass.ds((i + b) * PIECE, PIECE)],
                             piece_parts[:, b]).then_inc(s[f"parts_out{b}"], 16)
            for c in range(4):
                load0(c - c % 2, c % 2)
                if c < 2:
                    load_piece(0, c)
            with sp.Fori(2, CHUNKS // 2) as j:
                for b in range(2):
                    load0(j * 2, b)
                    store_parts(j * 2 - 4, b)
                    load_piece(j * 2 - 2, b)
            for c in range(CHUNKS - 4, CHUNKS):
                store_parts(c - c % 2, c % 2)
                if c < CHUNKS - 2:
                    load_piece(c - c % 2 + 2, c % 2)
            for b in range(2):
                sp.wait_ge(s[f"parts_out{b}"], 16 * (CHUNKS // 2))
            sp.wait_ge(s["memsets"], 1)
            sp.wait_ge(s["flag_set"], 1)
            for l in range(2):
                choose(sp, edge_sp, edge_sp_general, layers[l])
                n = ns[l + 1]
                sp.wait_ge(n0["base"], CHUNKS)

                def load(i, b):
                    if reused(i):
                        sp.wait_ge(n["variance"], i + (b - 1))
                        sp.sem_inc(s["tick"], 1)
                    sp.dma_start(rows_in[:, b], acc_v[l][:, chunk_cols(i, b), :]).then_inc(n[f"in{b}"], 16)
                chunks(sp, load)
            for b in range(2):
                sp.wait_ge(ns[2][f"out{b}"], 16 * (CHUNKS // 2))

        def gather_tile(g_out, idx, l, done):
            nc.gpsimd.indirect_dma_start(g_out, None, f_dram[l][:, :],
                                         bass.IndirectOffsetOnAxis(ap=idx, axis=0)).then_inc(done, 16)

        def edge_pool(pool, L):
            e = es[L.n]

            def body(g):
                b = g.b
                pool.wait_ge(e["loaded"][b], g.slot_count(32))
                pool.sem_inc(e["tick"], 1)
                if g.has(-UNROLL):
                    pool.wait_ge(e["prods"], g.times(PAIRS, -PAIRS * (UNROLL - 1)))
                    pool.sem_inc(e["tick"], 1)
                for t in range(TILES):
                    gather_tile(gath[:, b, t, :], ints[:, b, t:t + 1], L.n, e["gathered"][b])
            groups(pool, body)

        def edge_pool_general(pool, L):
            e = es[L.n]
            at, n = turns(L.deep)
            pool.wait_ge(e["acc_zeroed"], 16 * (ROWS // P // 3))
            with pool.Fori(0, GROUPS) as i:
                pool.wait_ge(e["loaded"][0], i * (32 + L.ea_counts) + (32 + L.ea_counts))
                pool.sem_inc(e["tick"], 1)
                for t in range(TILES):
                    gather_tile(gath[:, 0, t, :], ints[:, 0, t:t + 1], L.n, e["g_gathered"])
                for t in range(TILES):
                    pool.wait_ge(e["turn"], i * n + (1 + at[f"add{t}"]))
                    pool.sem_inc(e["tick"], 1)
                    nc.gpsimd.indirect_dma_start(
                        acc_dram[L.n][:, :], bass.IndirectOffsetOnAxis(ap=target[:, :], axis=0),
                        zsum[:, 0, :], None, compute_op=ALU.add).then_inc(e["added"], 16)
                    pool.wait_ge(e["added"], i * (16 * TILES) + 16 * (t + 1))
                    pool.sem_inc(e["turn"], 1)

        def base_rows(pool, k, own):
            n = ns[k]

            def pack(i, b):
                pool.wait_ge(n["normed"], i + (b + 1))
                pool.sem_inc(s["tick"], 1)
                nc.gpsimd.tensor_copy(vx[:, b].rearrange("p (t n) -> p t n", t=CH), xn[:, b, :, 0:DX]).then_inc(n["packed"], 1)

            def body(i, b):
                if k == 0:
                    pool.wait_ge(n[f"in{b}"], i * 8 + 16)
                else:
                    after = next_chunk(i, b)
                    if after:
                        pack(*after)
                pool.wait_ge(n["made"], i * CH + (b + 1) * CH)
                nc.gpsimd.tensor_tensor(base[:, chunk_cols(i, b), :], two[:, b, :, 1, :], own(b),
                                        ALU.add).then_inc(n["base"], 1)
            if k == 1:
                pack(0, 0)
            chunks(pool, body)

        @block.gpsimd
        def _(pool):
            base_rows(pool, 0, lambda b: rows_in[:, b, :, 0:D])
            pool.wait_ge(s["flag_set"], 1)
            for l in range(2):
                if l == 1:
                    base_rows(pool, 1, lambda b: xn[:, b])
                for b in range(2):
                    pool.wait_ge(ns[l][f"out{b}"], 16 * (CHUNKS // 2))
                choose(pool, edge_pool, edge_pool_general, layers[l])
            n2 = ns[2]
            pool.wait_ge(s["attr_in"], 16)

            def help_sums(i, b):
                pool.wait_ge(n2[f"in{b}"], i * 8 + 16)
                if reused(i):
                    pool.wait_ge(n2["made"], i + (b - 1))
                last, k = slice(CH - HELPED, CH), bass.ds((i + b) * CH + (CH - HELPED), HELPED)
                nc.gpsimd.tensor_tensor(resid[:, b, last, :], rows_in[:, b, last, 0:D],
                                        attr[:, k].unsqueeze(2).to_broadcast([P, HELPED, D]), ALU.mult).then_inc(n2["helped"], 1)
                pool.wait_ge(n2["helped"], i * 2 + (2 * b + 1))
                nc.gpsimd.tensor_tensor(resid[:, b, last, :], resid[:, b, last, :], base[:, k, :],
                                        ALU.add).then_inc(n2["helped"], 1)
            chunks(pool, help_sums)

        def narrow(ps, c):
            return ps.rearrange("p (t c j) -> p t c j", c=4, j=SLOTS)[:, :, c, :]

        def broad(ps, c):
            return ps[:, c * P:(c + 1) * P]

        def evacuate_b(cols):
            for rows, c in ((slice(0, DV), 2), (slice(DV, P), 3)):
                last = nc.scalar.activation(by_tile(cols, zB[rows, :]), cols(aggB_ps[rows, :], c), ACT.Copy)
            return last

        def evacuate_a(cols, bank_a):
            lo, hi = slice(0, 64), slice(64, 128)
            for out, rows, c in ((zA1[lo, :], lo, 3), (zA1[hi, :], hi, 2), (zA2[lo, :], hi, 0), (zA2[hi, :], hi, 1)):
                last = nc.scalar.activation(by_tile(cols, out), cols(bank_a[rows, :], c), ACT.Copy)
            return last

        def by_tile(cols, out):
            return out.rearrange("p (t j) -> p t j", j=SLOTS) if cols is narrow else out

        def activate(L, out, ps, fan_in):
            return nc.scalar.activation(out, ps[:, :], L.func, scale=fan_in ** -0.5)

        def edge_act(act, L):
            e = es[L.n]

            def hidden1(g):
                act.wait_ge(e["l1"], g.times(1, 1))
                if L.deep:
                    if g.has(-1):
                        act.wait_ge(e["l2"], g.times(1, 0))
                    activate(L, h1[:, :], hid1_ps, L.attrs).then_inc(e["h1"], 1)
                else:
                    if g.has(-2):
                        act.wait_ge(e["w"], g.times(PAIRS, -PAIRS))
                    activate(L, h2[:, g.b % 2, :], hid1_ps, L.attrs).then_inc(e["h2"], 1)

            def hidden2(g):
                act.wait_ge(e["l2"], g.times(1, 1))
                if g.has(-2):
                    act.wait_ge(e["w"], g.times(PAIRS, -PAIRS))
                activate(L, h2[:, g.b % 2, :], hid2_ps, MS).then_inc(e["h2"], 1)

            def evac(g):
                act.wait_ge(e["scattered"], g.times(PAIRS, PAIRS))
                if g.has(-1):
                    act.wait_ge(e["projected"], g.times(1, 0))
                evacuate_b(narrow).then_inc(e["evac_b"], 1)
                evacuate_a(narrow, aggA_ps[g.b % 2]).then_inc(e["evac"], 1)

            def zrows(g):
                act.wait_ge(e["projected"], g.times(1, 1))
                if g.has(-1):
                    act.wait_ge(e["combined"], g.times(1, 0))
                nc.scalar.activation(zrow[:, :], z_ps[:, 0:ZW], ACT.Copy).then_inc(e["z"], 1)

            def zsums(g):
                act.wait_ge(e["combined"], g.times(1, 1))
                if g.has(-UNROLL):
                    act.wait_ge(e["stored"], g.times(16, -16 * (UNROLL - 1)))
                nc.scalar.activation(zsum[:, g.b, :], z_ps[:, 0:ZW], ACT.Copy).then_inc(e["zsum"], 1)

            def body(g):
                if g.has(-1):
                    evac(g.plus(-1))
                if g.has(1):
                    hidden1(g.plus(1))
                if g.has(-1):
                    zrows(g.plus(-1))
                if g.has(1) and L.deep:
                    hidden2(g.plus(1))
                if g.has(-1):
                    zsums(g.plus(-1))
            hidden1(G(None, 0))
            if L.deep:
                hidden2(G(None, 0))
            groups(act, body)
            last = G(None, GROUPS - 1)
            evac(last)
            zrows(last)
            zsums(last)

        def edge_act_general(act, L):
            e = es[L.n]
            at, n = turns(L.deep)
            with act.Fori(0, GROUPS) as i:
                def turn(name):
                    act.wait_ge(e["turn"], i * n + (1 + at[name]))
                turn("h1")
                activate(L, h1[:, :] if L.deep else h2[:, 0, :], hid1_ps, L.attrs).then_inc(e["turn"], 1)
                if L.deep:
                    turn("h2")
                    activate(L, h2[:, 0, :], hid2_ps, MS).then_inc(e["turn"], 1)
                for t in range(TILES):
                    turn(f"evac{t}")
                    evacuate_b(broad)
                    evacuate_a(broad, aggA_ps[0]).then_inc(e["turn"], 1)
                    turn(f"z{t}")
                    nc.scalar.activation(zrow[:, :], z_ps[:, 0:ZW], ACT.Copy).then_inc(e["turn"], 1)
                    turn(f"zsum{t}")
                    nc.scalar.activation(zsum[:, 0, :], z_ps[:, 0:ZW], ACT.Copy).then_inc(e["turn"], 1)

        def scaled_rows(act, k, l, before_tile):
            n = ns[k]

            def body(i, b):
                if reused(i):
                    act.wait_ge(n[f"out{b}"], i * 8)
                    act.wait_ge(n["base"], i + (b - 1))
                    act.sem_inc(s["tick"], 1)
                for j in range(CH):
                    tile = b * CH + j
                    before_tile(i, b, j)
                    act.wait_ge(n["psum"], i * CH + (tile + 1))
                    attribute = attr[:, bass.ds((i + b) * CH + j, 1)]
                    of_vx = quad_ps[j // QUAD][:, j % QUAD * 2 * DX:(j % QUAD + 1) * 2 * DX]
                    nc.scalar.activation(two[:, b, j, :, 0:DX], of_vx.rearrange("p (a n) -> p a n", a=2), ACT.Copy, scale=attribute)
                    nc.scalar.activation(two[:, b, j, :, DX:D], row_ps[tile % 2][:, 0:2 * P].rearrange("p (a n) -> p a n", a=2),
                                         ACT.Copy, scale=attribute).then_inc(n["made"], 1)
                act.wait_ge(n["made"], i * CH + (b + 1) * CH)
                act.sem_inc(s["tick"], 1)
                act.dma_start(f_v[l][:, chunk_cols(i, b), :], two[:, b, :, 0, :]).then_inc(n[f"out{b}"], 16)
            return body

        def root(n, act, i, b):
            act.wait_ge(n["variance"], i + (b + 1))
            nc.scalar.activation(std[:, b, :], std[:, b, :], ACT.Sqrt).then_inc(n["rooted"], 1)

        @block.scalar
        def _(act):
            act.dma_start(attr[:, :], dram["attr"]).then_inc(s["attr_in"], 16)
            act.dma_start(dst_all, dram["dst_all"]).then_inc(s["dst_in"], 16)
            act.dma_start(first_all, dram["first_all"]).then_inc(s["dst_in"], 16)
            act.dma_start(bases[:, :], dram["bases"]).then_inc(s["bases_in"], 16)
            act.dma_start(wt[1][:, :], dram["w1"]).then_inc(s["weights_in1"], 16)
            act.wait_ge(s["attr_in"], 16)
            chunks(act, scaled_rows(act, 0, 0, lambda i, b, j: None))
            act.wait_ge(s["flag_set"], 1)
            choose(act, edge_act, edge_act_general, layers[0])

            n1 = ns[1]

            def turn_over(i, b, j):
                tile = b * CH + j
                act.wait_ge(n1["transposed"], i * CH + (tile + 1))
                if reused(i) or tile >= 2:
                    act.wait_ge(n1["psum"], i * CH + (tile - 1))
                if j % QUAD == 0:
                    q, rows = j // QUAD, slice(0, min(QUAD, CH - j) * DX)
                    nc.scalar.activation(tT2[rows, q, :], turn_quad_ps[q][rows, 0:P], ACT.Copy)
                nc.scalar.activation(tT1[:, tile % 2, :], turn_ps[tile % 2][:, 0:P], ACT.Copy).then_inc(n1["turned"], 1)

            def turn_over_next(i, b, j):
                if j == 0 and next_chunk(i, b):
                    root(n1, act, *next_chunk(i, b))
                after = next_tile(i, b, j)
                if after:
                    turn_over(*after)
            root(n1, act, 0, 0)
            turn_over(0, 0, 0)
            chunks(act, scaled_rows(act, 1, 1, turn_over_next))
            choose(act, edge_act, edge_act_general, layers[1])

            n2 = ns[2]

            def result(i, b):
                if reused(i):
                    act.wait_ge(n2[f"out{b}"], i * 8)
                act.wait_ge(n2["normed"], i + (b + 1))
                for j in range(CH):
                    last = nc.scalar.activation(xn[:, b, j, :], resid[:, b, j, :], ACT.Identity,
                                                bias=shift[:, b, j:j + 1], scale=rstd[:, b, j:j + 1])
                last.then_inc(n2["made"], 1)
                act.wait_ge(n2["made"], i + (b + 1))
                act.sem_inc(s["tick"], 1)
                act.dma_start(out_v[:, chunk_cols(i, b), :], xn[:, b]).then_inc(n2[f"out{b}"], 16)
                if next_chunk(i, b):
                    root(n2, act, *next_chunk(i, b))
            root(n2, act, 0, 0)
            chunks(act, result)

        def mm(out, lhsT, rhs, start=True, stop=True):
            return nc.tensor.matmul(out, lhsT, rhs, start=start, stop=stop)

        def project(L):
            w = wt[L.n]
            mm(z_ps[:, 0:ZW], zB[:, :], w[:, W_ZB:W_END], True, False)
            mm(z_ps[:, 2 * MV:ZW], zA1[:, :], w[:, W_ZA1:W_ZA2], False, False)
            return mm(z_ps[:, 0:2 * MV], zA2[:, :], w[:, W_ZA2:W_ZB], False, True)

        def weights_mm(L, out, h, q):
            return mm(out[:, 0:2 * WN], h[:, q * P:(q + 1) * P], wt[L.n][:, W_W3:W_ZA1])

        def first_hidden(L, b):
            if L.deep:
                return mm(hid1_ps[:, :], wh1[:, :], ea_parts[:, b, :])
            return mm(hid1_ps[:, :], wt[L.n][:, W_H1:W_H2], ea[:, b, :])

        def edge_pe(pe, L):
            e = es[L.n]

            def hidden1(g):
                pe.wait_ge(e["ea_in"][g.b], g.slot_count(L.ea_counts))
                if g.has(-1):
                    pe.wait_ge(e["h1" if L.deep else "h2"], g.times(1, 0))
                first_hidden(L, g.b).then_inc(e["l1"], 1)

            def hidden2(g):
                pe.wait_ge(e["h1"], g.times(1, 1))
                if g.has(-1):
                    pe.wait_ge(e["h2"], g.times(1, 0))
                mm(hid2_ps[:, :], wt[L.n][:, W_H2:W_W3], h1[:, :]).then_inc(e["l2"], 1)

            def edge_weights(g, q):
                if q == 0:
                    pe.wait_ge(e["h2"], g.times(1, 1))
                if g.j is not None or g.c * PAIRS + q >= 2:
                    pe.wait_ge(e["prods"], g.times(PAIRS, q - 1))
                weights_mm(L, w_ps[q % 2], h2[:, g.b % 2, :], q).then_inc(e["w"], 1)

            def scatter(g, q):
                if q == 0:
                    pe.wait_ge(e["prep"], g.times(PREP, PREP))
                    if g.has(-1):
                        pe.wait_ge(e["evac_b"], g.times(1, 0))
                    if g.has(-2):
                        pe.wait_ge(e["evac"], g.times(1, -1))
                pe.wait_ge(e["prods"], g.times(PAIRS, q + 1))
                for h in range(2):
                    t = 2 * q + h
                    o = slice(t * 4 * SLOTS, (t + 1) * 4 * SLOTS)
                    blocks = sel[:, g.b % 2, t, :, :].rearrange("p c j -> p (c j)")
                    mm(aggA_ps[g.b % 2][:, o], prod[:, q % 2, h, 0:P], blocks[:, 0:4 * SLOTS])
                    last = mm(aggB_ps[:, o], prod[:, q % 2, h, P:PN], blocks[:, SLOTS:NB * SLOTS])
                last.then_inc(e["scattered"], 1)

            def projection(g):
                pe.wait_ge(e["evac"], g.times(1, 1))
                if g.has(-1):
                    pe.wait_ge(e["zsum"], g.times(1, 0))
                project(L).then_inc(e["projected"], 1)

            def combine(g):
                pe.wait_ge(e["z"], g.times(1, 1))
                last = mm(z_ps[:, 0:ZW], place[:, g.b, :], zrow[:, :], True, not g.has(-1))
                if g.has(-1):
                    last = mm(z_ps[:, 0:ZW], carry[:, g.b, :], zsum[:, (g.b - 1) % UNROLL, :], False, True)
                last.then_inc(e["combined"], 1)

            def body(g):
                for q in range(PAIRS):
                    if q < PAIRS - 1:
                        edge_weights(g, q + 1)
                    elif g.has(1):
                        edge_weights(g.plus(1), 0)
                    scatter(g, q)
                    if q == 0 and g.has(-1):
                        projection(g.plus(-1))
                    if q == 1 and g.has(1) and L.deep:
                        hidden2(g.plus(1))
                    if q == 2 and g.has(-1):
                        combine(g.plus(-1))
                    if q == PAIRS - 1 and g.has(2):
                        hidden1(g.plus(2))
            hidden1(G(None, 0))
            if L.deep:
                hidden2(G(None, 0))
            hidden1(G(None, 1))
            edge_weights(G(None, 0), 0)
            groups(pe, body)
            last = G(None, GROUPS - 1)
            projection(last)
            combine(last)

        def edge_pe_general(pe, L):
            e = es[L.n]
            at, n = turns(L.deep)
            with pe.Fori(0, GROUPS) as i:
                def turn(name):
                    pe.wait_ge(e["turn"], i * n + (1 + at[name]))
                pe.wait_ge(e["loaded"][0], i * (32 + L.ea_counts) + (32 + L.ea_counts))
                pe.sem_inc(e["tick"], 1)
                turn("l1")
                first_hidden(L, 0).then_inc(e["turn"], 1)
                if L.deep:
                    turn("l2")
                    mm(hid2_ps[:, :], wt[L.n][:, W_H2:W_W3], h1[:, :]).then_inc(e["turn"], 1)
                for q in range(PAIRS):
                    turn(f"w{q}")
                    weights_mm(L, w_ps[0], h2[:, 0, :], q).then_inc(e["turn"], 1)
                    for h in range(2):
                        t = 2 * q + h
                        turn(f"drow{t}")
                        nc.tensor.transpose(z_ps[:, 0:P], spread[:, :], c_(C_IDENT, P)).then_inc(e["turn"], 1)
                        turn(f"scatter{t}")
                        blocks = wide[:, :, :].rearrange("p c j -> p (c j)")
                        mm(aggA_ps[0][:, :], prod[:, 0, h, 0:P], blocks[:, 0:4 * P])
                        mm(aggB_ps[:, :], prod[:, 0, h, P:PN], blocks[:, P:NB * P]).then_inc(e["turn"], 1)
                        turn(f"project{t}")
                        project(L).then_inc(e["turn"], 1)
                        turn(f"combine{t}")
                        mm(z_ps[:, 0:ZW], place[:, 0, :], zrow[:, :]).then_inc(e["turn"], 1)

        def node_mm(l, ps, T1):
            return mm(ps[:, 0:2 * P], T1, wt[l][:, W_N1:W_N2])

        def quad_mm(l, q, T2):
            cols = min(QUAD, CH - q * QUAD) * 2 * DX
            return mm(quad_ps[q][:, 0:cols], T2, wt[l][:, W_N2:W_N2 + cols])

        def quad_out(pe, n, i, b, q):
            if reused(i) or b > 0:
                pe.wait_ge(n["made"], i * CH + (b * CH - CH + min(CH, (q + 1) * QUAD)))

        @block.tensor
        def _(pe):
            pe.wait_ge(s["consts_in"], 16)
            pe.wait_ge(s["weights_scaled"], 1)
            n0 = ns[0]

            def chunk0(i, b):
                pe.wait_ge(n0[f"turned_in{b}"], i * 16 + 32)
                for j in range(CH):
                    tile = b * CH + j
                    if j % QUAD == 0:
                        quad_out(pe, n0, i, b, j // QUAD)
                        quad_mm(0, j // QUAD, xT2[:, b, j // QUAD, :])
                    if reused(i) or tile >= 2:
                        pe.wait_ge(n0["made"], i * CH + (tile - 1))
                    node_mm(0, row_ps[tile % 2], xT1[:, b, j, :]).then_inc(n0["psum"], 1)
            chunks(pe, chunk0)
            pe.wait_ge(s["span_step"], SPAN_STEPS)
            mm(z_ps[0:1, 0:1], worst[:, 11:12], ones[:, 0:1]).then_inc(s["span_sum"], 1)
            pe.wait_ge(s["flag_set"], 1)
            pe.wait_ge(s["weights_scaled"], 2)
            choose(pe, edge_pe, edge_pe_general, layers[0])
            n1 = ns[1]

            def turn_over(i, b, j):
                tile = b * CH + j
                if j == 0:
                    pe.wait_ge(n1["normed"], i + (b + 1))
                    pe.wait_ge(n1["packed"], i + (b + 1))
                if reused(i) or tile >= 2:
                    pe.wait_ge(n1["turned"], i * CH + (tile - 1))
                if j % QUAD == 0:
                    n = min(QUAD, CH - j) * DX
                    nc.tensor.transpose(turn_quad_ps[j // QUAD][0:n, 0:P], vx[:, b, j * DX:j * DX + n], c_(C_IDENT, P))
                nc.tensor.transpose(turn_ps[tile % 2][:, 0:P], xn[:, b, j, DX:D],
                                    c_(C_IDENT, P)).then_inc(n1["transposed"], 1)

            def chunk1(i, b):
                for j in range(CH):
                    after = next_tile(i, b, j)
                    if after:
                        turn_over(*after)
                    tile = b * CH + j
                    pe.wait_ge(n1["turned"], i * CH + (tile + 1))
                    if j % QUAD == 0:
                        quad_out(pe, n1, i, b, j // QUAD)
                        quad_mm(1, j // QUAD, tT2[:, j // QUAD, :])
                    if reused(i) or tile >= 2:
                        pe.wait_ge(n1["made"], i * CH + (tile - 1))
                    node_mm(1, row_ps[tile % 2], tT1[:, tile % 2, :]).then_inc(n1["psum"], 1)
            turn_over(0, 0, 0)
            chunks(pe, chunk1)
            choose(pe, edge_pe, edge_pe_general, layers[1])

        def vector_times_y(rows, y):
            return nc.vector.tensor_tensor(
                gy[:, :, :].rearrange("p t (c u) -> p t c u", c=3), rows[:, :, 0:DV].rearrange("p t (c u) -> p t c u", c=3),
                y[:, :, 0:3].unsqueeze(3).to_broadcast([P, TILES, 3, MV]), ALU.mult)

        def sum_xy(out):
            return nc.vector.tensor_tensor(out, gy[:, :, 0:MV], gy[:, :, MV:2 * MV], ALU.add)

        def sum_z(out):
            return nc.vector.tensor_tensor(out, out, gy[:, :, 2 * MV:DV], ALU.add)

        def pair_products(out, w, rows, dot):
            w3 = w[:, 0:2 * WN].rearrange("p (h n) -> p h n", h=2)
            nc.vector.tensor_tensor(out[:, :, 0:P].rearrange("p h (k u) -> p h k u", k=2),
                                    w3[:, :, 0:P].rearrange("p h (k u) -> p h k u", k=2),
                                    rows[:, :, DV:D].unsqueeze(2).to_broadcast([P, 2, 2, MS]), ALU.mult)
            nc.vector.tensor_tensor(out[:, :, P:P + DV].rearrange("p h (c u) -> p h c u", c=3),
                                    w3[:, :, P:P + MV].unsqueeze(2).to_broadcast([P, 2, 3, MV]),
                                    rows[:, :, 0:DV].rearrange("p h (c u) -> p h c u", c=3), ALU.mult)
            return nc.vector.tensor_tensor(out[:, :, P + DV:PN], w3[:, :, P + MV:WN], dot, ALU.mult)

        def edge_dve(dve, L):
            e = es[L.n]

            def prods(g, q):
                if q == 0:
                    dve.wait_ge(e["dots"], g.times(DOTS, DOTS))
                dve.wait_ge(e["w"], g.times(PAIRS, q + 1))
                if g.j is not None or g.c * PAIRS + q >= 2:
                    dve.wait_ge(e["scattered"], g.times(PAIRS, q - 1))
                pair_products(prod[:, q % 2], w_ps[q % 2], gath[:, g.b, 2 * q:2 * q + 2, :],
                              dots[:, g.b % 2, 2 * q:2 * q + 2, :]).then_inc(e["prods"], 1)

            def prep(g, part):
                b, d = g.b, g.b % 2

                def step(ins):
                    ins.then_inc(e["prep"], 1)

                def own(k):
                    dve.wait_ge(e["prep"], g.times(PREP, k))
                if part == 0:
                    dve.wait_ge(e["loaded"][b], g.slot_count(32))
                    if g.has(-2):
                        dve.wait_ge(e["scattered"], g.times(PAIRS, -PAIRS))
                    if g.has(-UNROLL):
                        dve.wait_ge(e["combined"], g.times(1, -(UNROLL - 1)))
                    window, window_before = (
                        (bases[:, (g.c + k):(g.c + k) + 1] if g.j is None else bases[:, bass.ds(g.j * UNROLL + (g.c + k), 1)])
                        for k in (0, -1 if g.has(-1) else 0))
                    step(nc.vector.tensor_tensor(rel[:, :], ints[:, b, TILES:2 * TILES],
                                                 ints[:, b, 2 * TILES:3 * TILES], ALU.subtract))
                    step(nc.vector.scalar_tensor_tensor(out=slot_col[:, :], in0=ints[:, b, 3 * TILES:NI],
                                                        scalar=c_(C_PMOD, 1), in1=window, op0=ALU.add, op1=ALU.subtract))
                    step(nc.vector.scalar_tensor_tensor(out=carry[:, b, 0:1], in0=window, scalar=c_(C_PART, 1),
                                                        in1=window_before, op0=ALU.subtract, op1=ALU.is_equal))
                    own(1)
                    step(nc.vector.tensor_tensor(
                        sel[:, d, :, NB - 1, :], rel[:, :].unsqueeze(2).to_broadcast([P, TILES, SLOTS]),
                        c_(C_SLOT, SLOTS).unsqueeze(1).to_broadcast([P, TILES, SLOTS]), ALU.is_equal))
                    own(2)
                    step(nc.vector.tensor_scalar(place[:, b, :], c_(C_SLOT, P), slot_col[:, 0:1], None, ALU.is_equal))
                else:
                    own(4)
                    step(nc.vector.tensor_tensor(
                        sel[:, d, :, 0:NB - 1, :],
                        sel[:, d, :, NB - 1, :].unsqueeze(2).to_broadcast([P, TILES, NB - 1, SLOTS]),
                        ysb[:, b].unsqueeze(3).to_broadcast([P, TILES, NB - 1, SLOTS]), ALU.mult))

            def dot(g, k):
                if k == 0:
                    dve.wait_ge(e["gathered"][g.b], g.slot_count(16 * TILES))
                    vector_times_y(gath[:, g.b], ysb[:, g.b]).then_inc(e["dots"], 1)
                else:
                    dve.wait_ge(e["dots"], g.times(DOTS, k))
                    (sum_xy if k == 1 else sum_z)(dots[:, g.b % 2]).then_inc(e["dots"], 1)

            def body(g):
                after = g.plus(1)
                for q in range(PAIRS):
                    prods(g, q)
                    if g.has(1):
                        if q < 2:
                            prep(after, q)
                        else:
                            dot(after, q - 2)
                        if q == 3:
                            dot(after, 2)
            first = G(None, 0)
            prep(first, 0)
            prep(first, 1)
            for k in range(DOTS):
                dot(first, k)
            groups(dve, body)

        def edge_dve_general(dve, L):
            e = es[L.n]
            at, n = turns(L.deep)
            with dve.Fori(0, GROUPS) as i:
                def turn(name):
                    dve.wait_ge(e["turn"], i * n + (1 + at[name]))

                def done(ins):
                    ins.then_inc(e["turn"], 1)
                turn("gy")
                dve.wait_ge(e["g_gathered"], i * (16 * TILES) + 16 * TILES)
                done(vector_times_y(gath[:, 0], ysb[:, 0]))
                turn("gd1")
                done(sum_xy(dots[:, 0]))
                turn("gd2")
                done(sum_z(dots[:, 0]))
                for q in range(PAIRS):
                    turn(f"prod{q}")
                    done(pair_products(prod[:, 0], w_ps[0], gath[:, 0, 2 * q:2 * q + 2, :], dots[:, 0, 2 * q:2 * q + 2, :]))
                    for t in (2 * q, 2 * q + 1):
                        dst = ints[:, 0, TILES + t:TILES + t + 1]
                        turn(f"spread{t}")
                        done(nc.vector.tensor_copy(spread[:, :], dst.to_broadcast([P, P])))
                        turn(f"prep{t}")
                        nc.vector.tensor_copy(slot_col[:, :], dst)
                        done(nc.vector.tensor_copy(dst_row[:, :], z_ps[:, 0:P]))
                        turn(f"prep_b{t}")
                        for c in range(4):
                            nc.vector.tensor_scalar(wide[:, c, :], c_(C_IDENT, P), ysb[:, 0, t, c:c + 1], None, ALU.mult)
                        nc.vector.tensor_copy(wide[:, 4, :], c_(C_IDENT, P))
                        nc.vector.tensor_tensor(to_trash[:, :], c_(C_TRASH, 1), slot_col[:, :], ALU.subtract)
                        done(nc.vector.tensor_scalar(place[:, 0, :], dst_row[:, :], slot_col[:, 0:1], None, ALU.is_equal))
                        turn(f"prep_c{t}")
                        done(nc.vector.tensor_tensor_reduce(
                            out=earlier[:, :], in0=place[:, 0, :], in1=c_(C_LOWER, P), scale=1.0, scalar=0.0,
                            op0=ALU.mult, op1=ALU.add, accum_out=dup[:, :]))
                        turn(f"prep_d{t}")
                        done(nc.vector.tensor_scalar(is_dup[:, :], dup[:, :], 0.5, None, ALU.is_gt))
                        turn(f"target{t}")
                        done(nc.vector.scalar_tensor_tensor(
                            out=target[:, :], in0=to_trash[:, :], scalar=is_dup[:, 0:1],
                            in1=slot_col[:, :], op0=ALU.mult, op1=ALU.add))

        def norm(dve, l):
            k = l + 1
            n = ns[k]
            own_sums = CH if l == 0 else CH - HELPED
            per = (2 if l == 0 else 1) + own_sums + CH + 1
            dve.wait_ge(ns[k - 1]["base"], CHUNKS)
            dve.wait_ge(s["attr_in"], 16)

            def moments(i, b):
                count = [0]

                def step(ins):
                    ins.then_inc(n["step"], 1)
                    count[0] += 1
                    return count[0]

                def own(c):
                    dve.wait_ge(n["step"], i * per + (b * per + c))
                dve.wait_ge(n[f"in{b}"], i * 8 + 16)
                if reused(i) and k == 2:
                    dve.wait_ge(n["made"], i + (b - 1))
                a_cols = attr[:, chunk_cols(i, b)]
                if l == 0:
                    own(step(nc.vector.tensor_tensor(gain[:, :], a_cols, a_cols, ALU.mult)))
                    a = step(nc.vector.tensor_tensor(gain[:, :].unsqueeze(2), gain[:, :].unsqueeze(2),
                                                     rows_in[:, b, :, D:ZW], ALU.mult))
                else:
                    a = step(nc.vector.tensor_copy(gain[:, :], a_cols))
                own(a)
                us = [step(nc.vector.scalar_tensor_tensor(
                    out=resid[:, b, j, :], in0=rows_in[:, b, j, 0:D], scalar=gain[:, j:j + 1],
                    in1=base[:, bass.ds((i + b) * CH + j, 1), :].rearrange("p a n -> p (a n)"),
                    op0=ALU.mult, op1=ALU.add)) for j in range(own_sums)]
                for j in range(CH):
                    if j < own_sums:
                        own(us[j])
                    elif j == own_sums:
                        dve.wait_ge(n["helped"], i * 2 + (2 * b + 2))
                    a = step(nc.vector.bn_stats(stats[:, j, :], resid[:, b, j, :]))
                own(a)
                dve.sem_inc(s["tick"], 1)
                for j in range(CH):
                    last = nc.vector.bn_aggr(mv[:, b, j, :], stats[:, j, :])
                own(step(last))
                nc.vector.tensor_scalar(std[:, b, :].unsqueeze(2), mv[:, b, :, 1:2], EPS, None,
                                        ALU.add).then_inc(n["variance"], 1)
                assert count[0] == per

            def apply(i, b):
                dve.wait_ge(n["rooted"], i + (b + 1))
                nc.vector.reciprocal(rstd[:, b, :], std[:, b, :]).then_inc(n["inverted"], 1)
                dve.wait_ge(n["inverted"], i + (b + 1))
                if k == 1:
                    if reused(i):
                        dve.wait_ge(n["base"], i + (b - 1))
                    for j in range(CH):
                        last = nc.vector.tensor_scalar(xn[:, b, j, :], resid[:, b, j, :], mv[:, b, j, 0:1],
                                                       rstd[:, b, j:j + 1], ALU.subtract, ALU.mult)
                else:
                    last = nc.vector.scalar_tensor_tensor(out=shift[:, b, :].unsqueeze(2), in0=mv[:, b, :, 0:1], scalar=-1.0,
                                                          in1=rstd[:, b, :].unsqueeze(2), op0=ALU.mult, op1=ALU.mult)
                last.then_inc(n["normed"], 1)

            def body(i, b):
                if k == 1:
                    after = next_chunk(i, b)
                    if after:
                        moments(*after)
                else:
                    moments(i, b)
                apply(i, b)
            if k == 1:
                moments(0, 0)
            chunks(dve, body)

        def look_at_dst(dve):
            count = [0]

            def link(ins):
                count[0] += 1
                ins.then_inc(s["span_step"], 1)
                dve.wait_ge(s["span_step"], count[0])

            def per_group(ap):
                return ap.rearrange("p (g t) -> p g t", t=TILES)

            def of_groups(lo):
                return bases[:, lo:lo + GROUPS].unsqueeze(2).to_broadcast([P, GROUPS, TILES])

            def extreme(k, ap, op):
                return nc.vector.tensor_reduce(worst[:, k:k + 1], ap, AXX, op)
            dve.wait_ge(s["dst_in"], 32)
            dve.wait_ge(s["bases_in"], 16)
            link(nc.vector.tensor_tensor(span, dst_all, first_all, ALU.subtract))
            extreme(0, span, ALU.max)
            link(extreme(1, span, ALU.min))
            link(nc.vector.tensor_tensor(per_group(span), per_group(dst_all), of_groups(1), ALU.subtract))
            link(extreme(2, span, ALU.max))
            link(nc.vector.tensor_tensor(per_group(span), per_group(dst_all), of_groups(0), ALU.subtract))
            link(extreme(3, span, ALU.min))
            link(nc.vector.tensor_tensor(span[:, 0:GROUPS], bases[:, 1:GROUPS + 1], bases[:, 0:GROUPS], ALU.subtract))
            link(extreme(4, span[:, 0:GROUPS], ALU.max))
            for a, lim, op in ((0, SLOTS - 0.5, ALU.is_gt), (1, -0.5, ALU.is_lt), (2, 0.5, ALU.is_gt),
                               (3, -0.5, ALU.is_lt)):
                nc.vector.tensor_scalar(worst[:, 5 + a:6 + a], worst[:, a:a + 1], lim, None, op)
            link(nc.vector.tensor_scalar(worst[:, 9:10], worst[:, 4:5], P - 0.5, None, ALU.is_gt))
            link(nc.vector.tensor_tensor(worst[:, 5:7], worst[:, 5:7], worst[:, 7:9], ALU.add))
            link(nc.vector.tensor_tensor(worst[:, 10:11], worst[:, 5:6], worst[:, 6:7], ALU.add))
            link(nc.vector.tensor_tensor(worst[:, 11:12], worst[:, 10:11], worst[:, 9:10], ALU.add))
            assert count[0] == SPAN_STEPS

        def split_hidden_weights(dve):
            count = [0]

            def link(ins):
                count[0] += 1
                ins.then_inc(s["w_split_step"], 1)
                dve.wait_ge(s["w_split_step"], count[0])
            w = wt[0][:, W_H1:W_H2]
            dve.wait_ge(s["consts_in"], 16)
            link(nc.vector.tensor_copy(w_parts[:, 0, :], w))
            link(nc.vector.tensor_tensor(w_rest[:, 0, :], w, w_parts[:, 0, :], ALU.subtract))
            link(nc.vector.tensor_copy(w_parts[:, 1, :], w_rest[:, 0, :]))
            link(nc.vector.tensor_tensor(w_parts[:, 2, :], w_rest[:, 0, :], w_parts[:, 1, :], ALU.subtract))
            link(nc.vector.tensor_scalar(w_sum[:, 0, :], w_parts[:, 0, :], c_(C_MASK, 1), None, ALU.mult))
            link(nc.vector.scalar_tensor_tensor(out=w_sum[:, 1, :], in0=w_parts[:, 1, :], scalar=c_(C_MASK + 1, 1),
                                                in1=w_sum[:, 0, :], op0=ALU.mult, op1=ALU.add))
            link(nc.vector.scalar_tensor_tensor(out=wh1[:, :], in0=w_parts[:, 2, :], scalar=c_(C_MASK + 2, 1),
                                                in1=w_sum[:, 1, :], op0=ALU.mult, op1=ALU.add))

        def split_piece(dve, i, b):
            def own(k):
                dve.wait_ge(s["split_step"], i * 3 + (b * 3 + k))
            dve.wait_ge(s[f"piece_in{b}"], i * 8 + 16)
            if reused(i):
                dve.wait_ge(s[f"parts_out{b}"], i * 8)
            x, (high, middle, low) = piece_in[:, b], (piece_parts[:, b, k] for k in range(3))
            nc.vector.tensor_copy(high, x).then_inc(s["split_step"], 1)
            own(1)
            nc.vector.tensor_tensor(rest[:, :], x, high, ALU.subtract).then_inc(s["split_step"], 1)
            own(2)
            nc.vector.tensor_copy(middle, rest[:, :]).then_inc(s["split_step"], 1)
            own(3)
            nc.vector.tensor_tensor(low, rest[:, :], middle, ALU.subtract).then_inc(s["split"], 1)

        @block.vector
        def _(dve):
            for L in layers:
                dve.wait_ge(s[f"weights_in{L.n}"], 16)
                w, own_s, own_v = wt[L.n], MS ** -0.5, MV ** -0.5
                for f, c in ((1.0, 0), (L.own_scale, 1)):
                    a = W_N1 + c * P
                    nc.vector.tensor_scalar(w[:, a:a + 2 * MV], w[:, a:a + 2 * MV], own_v * f, None, ALU.mult)
                    nc.vector.tensor_scalar(w[:, a + 2 * MV:a + P], w[:, a + 2 * MV:a + P], own_s * f, None, ALU.mult)
                    of_vx = w[:, W_N2:W_H1].rearrange("p (q a n) -> p q a n", q=QUAD, a=2)[:, :, c, :]
                    last = nc.vector.tensor_scalar(of_vx, of_vx, own_v * f, None, ALU.mult)
                if L.n == 0:
                    last.then_inc(s["weights_scaled"], 1)
                    split_hidden_weights(dve)
                nc.vector.tensor_scalar(w[:, W_ZA1:W_ZB], w[:, W_ZA1:W_ZB], L.scale, None, ALU.mult)
                nc.vector.tensor_scalar(w[0:DV, W_ZB:W_END], w[0:DV, W_ZB:W_END], L.scale, None, ALU.mult)
                last = nc.vector.tensor_scalar(w[DV:P, W_ZB:W_END], w[DV:P, W_ZB:W_END], L.scale * 3 ** -0.5, None, ALU.mult)
            last.then_inc(s["weights_scaled"], 1)
            nc.vector.memset(zeros[:, :], 0.0)
            nc.vector.memset(ones[:, :], 1.0)
            nc.vector.memset(tT2[:, :, :], 0.0)
            nc.vector.memset(carry[:, :, :], 0.0)
            nc.vector.memset(ea[:, :, :], 0.0).then_inc(s["memsets"], 1)
            dve.wait_ge(s["consts_in"], 16)
            look_at_dst(dve)
            chunks(dve, lambda i, b: split_piece(dve, i, b))
            dve.wait_ge(s["span_sum"], 1)
            nc.vector.tensor_scalar(flag[0:1, :], z_ps[0:1, 0:1], 0.5, None, ALU.is_lt).then_inc(s["flag_set"], 1)
            dve.wait_ge(s["flag_set"], 1)
            for l in range(2):
                choose(dve, edge_dve, edge_dve_general, layers[l])
                norm(dve, l)


def kernel(**inputs):
    import numpy as np
    import concourse.bacc as bacc
    from concourse.bass_utils import run_bass_kernel_spmd as run

    arr = {k: np.asarray(v) for k, v in inputs.items()}
    pad = GROUPS * GROUP - N_EDGES
    x = np.pad(np.concatenate([arr["x"][:, MS:].reshape(-1, MV, 3).transpose(0, 2, 1).reshape(-1, DV),
                               arr["x"][:, :MS]], 1), ((0, P * NT - N_NODES), (0, 0)))
    attr = np.pad(arr["node_vec1"], ((0, P * NT - N_NODES), (0, 0))).reshape(P, NT)
    turned = x.reshape(P, NT, D).transpose(2, 1, 0)
    quads = np.pad(turned[:DX].reshape(DX, CHUNKS, CH, P), ((0, 0), (0, 0), (0, QUADS * QUAD - CH), (0, 0)))
    quads = quads.reshape(DX, CHUNKS * QUADS, QUAD, P).transpose(2, 0, 1, 3).reshape(P, -1, P)
    src = np.pad(arr["src"], (0, pad)).reshape(GROUPS, TILES, P)
    dst = np.pad(arr["dst"], (0, pad), mode="edge").reshape(GROUPS, TILES, P)
    first = np.broadcast_to(dst[:, None, :, 0], (GROUPS, P, TILES))
    slot_first = np.repeat(dst[:, :, 0], SLOTS, 1)[:, :, None]
    ints = np.concatenate([src.transpose(0, 2, 1), dst.transpose(0, 2, 1), first, slot_first], 2)
    ends = np.zeros(1, dst.dtype), np.full(1, N_NODES, dst.dtype)
    bases = np.broadcast_to(np.concatenate([ends[0], dst[1:, 0, 0], ends[1]]), (P, GROUPS + 1))
    y = np.pad(arr["edge_attr_4"][:, [1, 2, 3, 0]], ((0, pad), (0, 0))).reshape(GROUPS, TILES, P, 4).transpose(0, 2, 1, 3)

    def hidden_in(a):
        n = a.shape[1]
        a = np.pad(a, ((0, pad), (0, 0))).reshape(GROUPS, PAIRS, 2, P, n)
        return a.transpose(0, 2, 4, 1, 3).reshape(GROUPS, 2 * n, HID)
    p = np.arange(P)
    consts = np.zeros((P, C_END), np.float32)
    consts[:, C_SLOT:C_SLOT + P] = p
    consts[:, C_PMOD] = p % SLOTS
    consts[:, C_TRASH] = TRASH + p
    consts[:, C_PART] = p
    consts[:, C_LOWER:C_LOWER + P] = p[:, None] > p[None, :]
    consts[:, C_IDENT:C_MASK] = np.eye(P)
    consts[:, C_MASK:C_END] = np.repeat(W_PARTS, P // len(W_PARTS))[:, None] == np.arange(3)

    def weights(l, l1_s, l1_v, sc_s, sc_v, h, w3, l2_s, l2_v, a):
        w = np.zeros((P, W_END), arr["x"].dtype)

        def put(r, c, block):
            w[r:r + block.shape[0], c:c + block.shape[1]] = block
        for k, (ws, wv) in enumerate(((l1_s, l1_v), (sc_s, sc_v))):
            for v in range(2):
                put(MV * v, W_N1 + k * P + MV * v, wv)
            put(2 * MV, W_N1 + k * P + 2 * MV, ws)
            for q in range(QUAD):
                put(MV * q, W_N2 + (2 * q + k) * DX, wv)
        for half in range(2):
            for block in range(len(W_PARTS) if l == 0 else 1):
                put(h[0].shape[0] * (2 * block + half), W_H1 + MS * half, h[0])
            if len(h) > 1:
                put(MS * half, W_H2 + MS * half, h[1])
            put(MS * half, W_W3 + WN * half, w3)
            put(MS * half, W_ZA2 + MV * half, l2_v[:MS])
        put(MS, W_ZA1, l2_v[:MS])
        put(0, W_ZA1 + MV, l2_s[:MS])
        for v in range(3):
            put(MV * v, W_ZB + MV * v, l2_v[MS:])
        put(DV, W_ZB + DV, l2_s[MS:])
        if a is not None:
            put(0, W_ZA1 + MV + MS, a[:MS])
            put(DV, W_ZB + D, a[MS:])
        return w
    g = lambda l, n: arr[f"L{l}_gnn_{n}"]
    arrays = {
        "x": x, "attr": attr, "xT1": turned[DX:D], "xT2": quads, "ints": ints, "y": y, "bases": bases,
        "dst_all": dst.transpose(2, 0, 1).reshape(P, -1), "first_all": first.transpose(1, 0, 2).reshape(P, -1),
        "ea8": hidden_in(arr["edge_attr_8"]), "ea16": hidden_in(arr["edge_attr_16"]), "consts": consts,
        "w0": weights(0, g(0, "Wl1_0"), g(0, "Wl1_1"), g(0, "Wsc0"), g(0, "Wsc1"), [g(0, "Wfc1"), g(0, "Wfc2")],
                      g(0, "Wfc3"), g(0, "Wl2_s"), g(0, "Wl2_v"), g(0, "Wa")),
        "w1": weights(1, g(1, "W_l1_0"), g(1, "W_l1_1"), g(1, "W_sc0"), g(1, "W_sc1"), [g(1, "fc_W1")],
                      g(1, "fc_W2"), g(1, "W_l2_0"), g(1, "W_l2_1"), None),
    }
    nc = bacc.Bacc("TRN2", target_bir_lowering=False, num_devices=1)
    arrays = {f"in_{k}": np.ascontiguousarray(v) for k, v in arrays.items()}
    dram = {k[3:]: nc.dram_tensor(k, v.shape, mybir.dt.from_np(v.dtype), kind="ExternalInput").ap()
            for k, v in arrays.items()}
    dram["out"] = nc.dram_tensor("out_x", (P * NT, D), F32, kind="ExternalOutput").ap()
    build(nc, dram)
    got = run(nc, [arrays], core_ids=[0]).results[0]["out_x"][:N_NODES]
    return np.concatenate([got[:, DV:], got[:, :DV].reshape(-1, 3, MV).transpose(0, 2, 1).reshape(-1, DV)], 1)
```
